# Optimizing a Trainium2 kernel written in Bass

```python
import numpy as np
import jax
import jax.numpy as jnp

def _softmax(x, axis=-1):
    return jax.nn.softmax(x, axis=axis)

def _gelu(x):
    return jax.nn.gelu(x, approximate=True)

def _silu(x):
    return jax.nn.silu(x)

def _sigmoid(x):
    return jax.nn.sigmoid(x)

def _layernorm(x, axis=-1, eps=1e-05):
    m = jnp.mean(x, axis=axis, keepdims=True)
    v = jnp.var(x, axis=axis, keepdims=True)
    return (x - m) / jnp.sqrt(v + eps)

def _scatter_add(tgt, idx, src, axis=0):
    return tgt.at[idx].add(src)

def _segment_sum(src, seg, n):
    return jax.ops.segment_sum(src, seg, n)
kernel_name = 'mk_cond_seq_d4_seqx_r4_9f18e1'

def setup_inputs(seed: int=0):
    np.random.seed(seed)
    _w = jnp.asarray

    def _rec_inputs():
        import jax
        import jax.numpy as jnp
        _rk = jax.random.key(seed)
        x = 0.5 + 0.2887 * jax.random.normal(jax.random.fold_in(_rk, 1), (4, 512, 512), jnp.float32)
        _lenS = 512 - jax.random.randint(jax.random.fold_in(_rk, 7), (4,), 0, max(1, 512 // 4) + 1, jnp.int32)
        _lenS2 = 512 - jax.random.randint(jax.random.fold_in(_rk, 8), (4,), 0, max(1, 512 // 4) + 1, jnp.int32)
        itok_B_17_1546 = jax.random.randint(jax.random.fold_in(_rk, 12), (4,), 17, 1547, jnp.int32)
        itok_B_1_2 = jax.random.randint(jax.random.fold_in(_rk, 13), (4,), 1, 3, jnp.int32)
        return (x, itok_B_17_1546, itok_B_1_2, _lenS)
    x, itok_B_17_1546, itok_B_1_2, _lenS = _rec_inputs()

    def _L0_cond_setup():
        import jax, jax.numpy as jnp
        import numpy as np
        B, T, V = (8, 128, 512)
        H = 4 * V
        key = jax.random.key(seed)
        ks = jax.random.split(key, 16)
        s = lambda n: 1.0 / np.sqrt(n)
        inp = {'x': jax.random.uniform(ks[0], (B, T, V), dtype=jnp.float32), 'lens': jax.random.randint(ks[1], (B,), 1, T, dtype=jnp.int64), 'target_codes': jax.random.randint(ks[2], (B,), 0, V, dtype=jnp.int64), 'Wq': jax.random.normal(ks[3], (V, V), jnp.float32) * s(V), 'Wk': jax.random.normal(ks[4], (V, V), jnp.float32) * s(V), 'Wv': jax.random.normal(ks[5], (V, V), jnp.float32) * s(V), 'Wp': jax.random.normal(ks[6], (V, V), jnp.float32) * s(V), 'bp': jnp.zeros((V,), jnp.float32), 'cW1': jax.random.normal(ks[7], (V, H), jnp.float32) * s(V), 'cb1': jnp.zeros((H,), jnp.float32), 'cW2': jax.random.normal(ks[8], (H, V), jnp.float32) * s(H), 'cb2': jnp.zeros((V,), jnp.float32), 'mW1': jax.random.normal(ks[9], (2 * V, H), jnp.float32) * s(2 * V), 'mb1': jnp.zeros((H,), jnp.float32), 'mW2': jax.random.normal(ks[10], (H, V), jnp.float32) * s(H), 'mb2': jnp.zeros((V,), jnp.float32)}
        return inp
    _L0_cond_all = _L0_cond_setup()
    _L0_cond_in = {k: v for k, v in _L0_cond_all.items() if k in ('Wq', 'Wk', 'Wv', 'Wp', 'bp', 'cW1', 'cb1', 'cW2', 'cb2', 'mW1', 'mb1', 'mW2', 'mb2')}
    del _L0_cond_all

    def _L1_cond_setup():
        import jax, jax.numpy as jnp
        import numpy as np
        B, S, H = (8, 512, 512)
        BN = 256
        E = 3
        LN_EPS = 1e-05
        key = jax.random.key(seed)
        ks = jax.random.split(key, 8)
        stream = jax.random.randint(ks[0], (B,), 0, E, dtype=jnp.int32)
        hidden_states = jax.random.normal(ks[1], (B, S, H), dtype=jnp.float32)
        W_down = jax.random.normal(ks[2], (E, H, BN), dtype=jnp.float32) * 0.02
        b_down = jnp.zeros((E, BN), dtype=jnp.float32)
        W_up = jax.random.normal(ks[3], (E, BN, H), dtype=jnp.float32) * 0.02
        b_up = jnp.zeros((E, H), dtype=jnp.float32)
        ln_w = jnp.ones((E, H), dtype=jnp.float32)
        ln_b = jnp.zeros((E, H), dtype=jnp.float32)
        return {'stream': stream, 'hidden_states': hidden_states, 'W_down': W_down, 'b_down': b_down, 'W_up': W_up, 'b_up': b_up, 'ln_w': ln_w, 'ln_b': ln_b}
    _L1_cond_all = _L1_cond_setup()
    _L1_cond_in = {k: v for k, v in _L1_cond_all.items() if k in ('W_down', 'b_down', 'W_up', 'b_up', 'ln_w', 'ln_b')}
    del _L1_cond_all

    def _L2_cond_setup():
        import jax, jax.numpy as jnp
        import numpy as np
        H = 512
        K = 256
        R = 3
        B = 8
        S = 512
        LN_EPS = 1e-05
        key = jax.random.key(seed)
        ks = jax.random.split(key, 8)
        sd_d = 1.0 / np.sqrt(H)
        sd_u = 1.0 / np.sqrt(K)
        return {'role': jax.random.randint(ks[0], (B,), 0, R), 'hidden_states': jax.random.normal(ks[1], (B, S, H), dtype=jnp.float32), 'W_down': jax.random.uniform(ks[2], (R, H, K), jnp.float32, -sd_d, sd_d), 'b_down': jax.random.uniform(ks[3], (R, K), jnp.float32, -sd_d, sd_d), 'W_up': jax.random.uniform(ks[4], (R, K, H), jnp.float32, -sd_u, sd_u), 'b_up': jax.random.uniform(ks[5], (R, H), jnp.float32, -sd_u, sd_u), 'gamma': jnp.ones((R, H), jnp.float32), 'beta': jnp.zeros((R, H), jnp.float32)}
    _L2_cond_all = _L2_cond_setup()
    _L2_cond_in = {k: v for k, v in _L2_cond_all.items() if k in ('W_down', 'b_down', 'W_up', 'b_up', 'gamma', 'beta')}
    del _L2_cond_all

    def _L3_cond_setup():
        import jax, jax.numpy as jnp
        import numpy as np
        H = 512
        K = 256
        R = 3
        B = 8
        S = 512
        LN_EPS = 1e-05
        key = jax.random.key(seed)
        ks = jax.random.split(key, 8)
        sd_d = 1.0 / np.sqrt(H)
        sd_u = 1.0 / np.sqrt(K)
        return {'role': jax.random.randint(ks[0], (B,), 0, R), 'hidden_states': jax.random.normal(ks[1], (B, S, H), dtype=jnp.float32), 'W_down': jax.random.uniform(ks[2], (R, H, K), jnp.float32, -sd_d, sd_d), 'b_down': jax.random.uniform(ks[3], (R, K), jnp.float32, -sd_d, sd_d), 'W_up': jax.random.uniform(ks[4], (R, K, H), jnp.float32, -sd_u, sd_u), 'b_up': jax.random.uniform(ks[5], (R, H), jnp.float32, -sd_u, sd_u), 'gamma': jnp.ones((R, H), jnp.float32), 'beta': jnp.zeros((R, H), jnp.float32)}
    _L3_cond_all = _L3_cond_setup()
    _L3_cond_in = {k: v for k, v in _L3_cond_all.items() if k in ('W_down', 'b_down', 'W_up', 'b_up', 'gamma', 'beta')}
    del _L3_cond_all
    return {'x': x, 'itok_B_17_1546': itok_B_17_1546, 'itok_B_1_2': itok_B_1_2, '_lenS': _lenS, 'L0_cond_Wq': _L0_cond_in['Wq'], 'L0_cond_Wk': _L0_cond_in['Wk'], 'L0_cond_Wv': _L0_cond_in['Wv'], 'L0_cond_Wp': _L0_cond_in['Wp'], 'L0_cond_bp': _L0_cond_in['bp'], 'L0_cond_cW1': _L0_cond_in['cW1'], 'L0_cond_cb1': _L0_cond_in['cb1'], 'L0_cond_cW2': _L0_cond_in['cW2'], 'L0_cond_cb2': _L0_cond_in['cb2'], 'L0_cond_mW1': _L0_cond_in['mW1'], 'L0_cond_mb1': _L0_cond_in['mb1'], 'L0_cond_mW2': _L0_cond_in['mW2'], 'L0_cond_mb2': _L0_cond_in['mb2'], 'L1_cond_W_down': _L1_cond_in['W_down'], 'L1_cond_b_down': _L1_cond_in['b_down'], 'L1_cond_W_up': _L1_cond_in['W_up'], 'L1_cond_b_up': _L1_cond_in['b_up'], 'L1_cond_ln_w': _L1_cond_in['ln_w'], 'L1_cond_ln_b': _L1_cond_in['ln_b'], 'L2_cond_W_down': _L2_cond_in['W_down'], 'L2_cond_b_down': _L2_cond_in['b_down'], 'L2_cond_W_up': _L2_cond_in['W_up'], 'L2_cond_b_up': _L2_cond_in['b_up'], 'L2_cond_gamma': _L2_cond_in['gamma'], 'L2_cond_beta': _L2_cond_in['beta'], 'L3_cond_W_down': _L3_cond_in['W_down'], 'L3_cond_b_down': _L3_cond_in['b_down'], 'L3_cond_W_up': _L3_cond_in['W_up'], 'L3_cond_b_up': _L3_cond_in['b_up'], 'L3_cond_gamma': _L3_cond_in['gamma'], 'L3_cond_beta': _L3_cond_in['beta']}

def reference(x, itok_B_17_1546, itok_B_1_2, _lenS, L0_cond_Wq, L0_cond_Wk, L0_cond_Wv, L0_cond_Wp, L0_cond_bp, L0_cond_cW1, L0_cond_cb1, L0_cond_cW2, L0_cond_cb2, L0_cond_mW1, L0_cond_mb1, L0_cond_mW2, L0_cond_mb2, L1_cond_W_down, L1_cond_b_down, L1_cond_W_up, L1_cond_b_up, L1_cond_ln_w, L1_cond_ln_b, L2_cond_W_down, L2_cond_b_down, L2_cond_W_up, L2_cond_b_up, L2_cond_gamma, L2_cond_beta, L3_cond_W_down, L3_cond_b_down, L3_cond_W_up, L3_cond_b_up, L3_cond_gamma, L3_cond_beta):
    import jax
    import jax.numpy as jnp

    def _L0_cond_ref(x, lens, target_codes, Wq, Wk, Wv, Wp, bp, cW1, cb1, cW2, cb2, mW1, mb1, mW2, mb2):
        import jax, jax.numpy as jnp
        import numpy as np
        B, T, V = (8, 128, 512)
        H = 4 * V
        scale = V ** (-0.5)
        q = x @ Wq
        k = x @ Wk
        v = x @ Wv
        attn = jnp.einsum('btd,bTd->btT', q, k) * scale
        attn = jax.nn.softmax(attn, axis=-1)
        attn_out = jnp.einsum('btT,bTd->btd', attn, v) @ Wp + bp
        target_embed = jax.nn.one_hot(target_codes, V, dtype=x.dtype)[:, None, :]
        cms_out = jax.nn.gelu(attn_out @ cW1 + cb1, approximate=False) @ cW2 + cb2
        cms_out = cms_out + target_embed
        concat = jnp.concatenate([attn_out, cms_out], axis=-1)
        modifier = jax.nn.gelu(concat @ mW1 + mb1, approximate=False) @ mW2 + mb2
        out = jnp.clip(x + cms_out + modifier, 0.0, 1.0)
        return out

    def _L1_cond_ref(stream, hidden_states, W_down, b_down, W_up, b_up, ln_w, ln_b):
        import jax, jax.numpy as jnp
        import numpy as np
        B, S, H = (8, 512, 512)
        BN = 256
        E = 3
        LN_EPS = 1e-05
        Wd = W_down[stream]
        bd = b_down[stream]
        Wu = W_up[stream]
        bu = b_up[stream]
        g = ln_w[stream]
        b = ln_b[stream]
        residual = hidden_states
        h = jnp.einsum('bsh,bhk->bsk', hidden_states, Wd) + bd[:, None, :]
        h = jax.nn.gelu(h, approximate=False)
        h = jnp.einsum('bsk,bkh->bsh', h, Wu) + bu[:, None, :]
        h = residual + h
        mean = jnp.mean(h, axis=-1, keepdims=True)
        var = jnp.mean(jnp.square(h - mean), axis=-1, keepdims=True)
        h = (h - mean) * jax.lax.rsqrt(var + LN_EPS)
        return h * g[:, None, :] + b[:, None, :]

    def _L2_cond_ref(role, hidden_states, W_down, b_down, W_up, b_up, gamma, beta):
        import jax, jax.numpy as jnp
        import numpy as np
        H = 512
        K = 256
        R = 3
        B = 8
        S = 512
        LN_EPS = 1e-05
        h = jnp.einsum('bsh,bhk->bsk', hidden_states, W_down[role]) + b_down[role][:, None, :]
        h = jax.nn.gelu(h, approximate=False)
        u = jnp.einsum('bsk,bkh->bsh', h, W_up[role]) + b_up[role][:, None, :]
        y = hidden_states + u
        mean = jnp.mean(y, axis=-1, keepdims=True)
        var = jnp.mean(jnp.square(y - mean), axis=-1, keepdims=True)
        yn = (y - mean) * jax.lax.rsqrt(var + LN_EPS)
        return yn * gamma[role][:, None, :] + beta[role][:, None, :]

    def _L3_cond_ref(role, hidden_states, W_down, b_down, W_up, b_up, gamma, beta):
        import jax, jax.numpy as jnp
        import numpy as np
        H = 512
        K = 256
        R = 3
        B = 8
        S = 512
        LN_EPS = 1e-05
        h = jnp.einsum('bsh,bhk->bsk', hidden_states, W_down[role]) + b_down[role][:, None, :]
        h = jax.nn.gelu(h, approximate=False)
        u = jnp.einsum('bsk,bkh->bsh', h, W_up[role]) + b_up[role][:, None, :]
        y = hidden_states + u
        mean = jnp.mean(y, axis=-1, keepdims=True)
        var = jnp.mean(jnp.square(y - mean), axis=-1, keepdims=True)
        yn = (y - mean) * jax.lax.rsqrt(var + LN_EPS)
        return yn * gamma[role][:, None, :] + beta[role][:, None, :]
    x = _L0_cond_ref(x, _lenS, itok_B_17_1546, L0_cond_Wq, L0_cond_Wk, L0_cond_Wv, L0_cond_Wp, L0_cond_bp, L0_cond_cW1, L0_cond_cb1, L0_cond_cW2, L0_cond_cb2, L0_cond_mW1, L0_cond_mb1, L0_cond_mW2, L0_cond_mb2)
    x = _L1_cond_ref(itok_B_1_2, x, L1_cond_W_down, L1_cond_b_down, L1_cond_W_up, L1_cond_b_up, L1_cond_ln_w, L1_cond_ln_b)
    x = _L2_cond_ref(itok_B_1_2, x, L2_cond_W_down, L2_cond_b_down, L2_cond_W_up, L2_cond_b_up, L2_cond_gamma, L2_cond_beta)
    x = _L3_cond_ref(itok_B_1_2, x, L3_cond_W_down, L3_cond_b_down, L3_cond_W_up, L3_cond_b_up, L3_cond_gamma, L3_cond_beta)
    return x

_drawn_inputs = setup_inputs


def setup_inputs(seed=0):
    import zlib

    import numpy as np

    out = dict(_drawn_inputs(seed))
    spreads = {'L0_cond_bp': (0.0, 0.1),
     'L0_cond_cb1': (0.0, 0.1),
     'L0_cond_cb2': (0.0, 0.1),
     'L0_cond_mb1': (0.0, 0.1),
     'L0_cond_mb2': (0.0, 0.1),
     'L1_cond_b_down': (0.0, 0.1),
     'L1_cond_b_up': (0.0, 0.1),
     'L1_cond_ln_w': (1.0, 0.2),
     'L1_cond_ln_b': (0.0, 0.1),
     'L2_cond_gamma': (1.0, 0.2),
     'L2_cond_beta': (0.0, 0.1),
     'L3_cond_gamma': (1.0, 0.2),
     'L3_cond_beta': (0.0, 0.1)}
    factors = {'L0_cond_Wq': 8.0, 'L0_cond_Wk': 8.0, 'L2_cond_b_down': 7.194, 'L3_cond_b_down': 7.015}
    for name, (base, spread) in spreads.items():
        noise = np.random.default_rng([zlib.crc32(name.encode()), seed]).standard_normal(out[name].shape)
        drawn = base * np.exp(spread * noise) if base else spread * noise
        out[name] = jnp.asarray(drawn.astype(out[name].dtype))
    for name, factor in factors.items():
        out[name] = (out[name] * factor).astype(out[name].dtype)
    return out
```

```python
from contextlib import ExitStack

import concourse.bass as bass
from concourse import mybir

F32 = mybir.dt.float32
F32R = mybir.dt.float32r
I32 = mybir.dt.int32
ALU = mybir.AluOpType
ACT = mybir.ActivationFunctionType
AX = mybir.AxisListType

P = 128
B = 4
S = 512
V = 512
H = 4 * V
KB = 256
LAYERS = 3
EXPERTS = 3
DT = V // P
MT = KB // P
HT = H // P
SCALE = V ** -0.5
EPS = 1e-5
W1 = DT * P + V
W2 = 2 * DT * P + V
NSLOT = 4
BANKS = 8
KiB = 1024


def build(nc, wts, xin, bias_in, codes_in, experts_in, mlp1, mlp2, wd_all, wu_all, pp_all, gb_all,
          bup_all, out):
    ctx = ExitStack()
    with ctx:
        base = -(-nc.sbuf_base // 64) * 64

        def at(name, kib, shape, dt=F32):
            return nc.alloc_sbuf_tensor_at(name, shape, dt, offset=base + int(kib * KiB))

        def sem(name):
            return ctx.enter_context(nc.semaphore(name))

        a_all = at("a_all", 0, [P, B, 2, DT, S], F32R)
        wqT = at("wqT", 0, [P, 2, DT, V], F32R)
        wkT = at("wkT", 16, [P, 2, DT, V], F32R)
        wvT = at("wvT", 32, [P, 2, DT, V], F32R)
        xrows = at("xrows", 48, [P, DT, V])
        g_w = at("g_w", 64, [P, 2, DT, V], F32R)
        vp_w = at("vp_w", 80, [P, 2, DT, V], F32R)
        xT = at("xT", 96, [P, 2, DT, S], F32R)
        uT = at("uT", 112, [P, 2, DT, S], F32R)
        v_n = at("v_n", 128, [P, 2, DT, V], F32R)
        pT = at("pT", 144, [P, 2, DT, S], F32R)
        wp_s = at("wp_s", 144, [P, 2, DT, V], F32R)
        res = at("res", 160, [P, B, DT, S])
        w_raw4 = at("w_raw4", 160, [P, 4, DT, V])
        probs = at("probs", 192, [P, DT, S])
        w_hl = [at(f"w_hl{i}", 64 + 12 * i, [P, 2, W2], F32R) for i in range(NSLOT)]
        cms = at("cms", 112, [P, 2, DT, S], F32R)
        g_hl = [at(f"g_hl{i}", 128 + 4 * i, [P, 2, S], F32R) for i in range(NSLOT)]
        raw = [at(f"raw{i}", k, [P, W2]) for i, k in enumerate((200, 192, 144, 150))]
        gf = [at(f"gf{i}", 156 + 2 * i, [P, S]) for i in range(2)]
        yT = [at(f"yT{b}", 16 * b, [P, 2, DT, S], F32R) for b in range(B)]
        wd = [at(f"wd{i}", 64 + 8 * i, [P, 2, DT, KB], F32R) for i in range(2)]
        bup0 = at("bup0", 80, [P, B, V])
        yf = [at(f"yf{i}", 80 + 2 * i, [P, S]) for i in range(2)]
        wu = [at(f"wu{i}", 88 + 8 * i, [P, 2, MT, V], F32R) for i in range(2)]
        z = [at("z0", 104, [P, DT, V]), at("z1", 136, [P, DT, V])]
        h_hl = [at(f"h_hl{i}", 112 + 8 * i, [P, 2, MT, S], F32R) for i in range(2)]
        bc = [at("bc0", 148, [P, 4, V]), at("bc1", 128, [P, 4, V])]
        hf = [at(f"hf{i}", 156 + 2 * i, [P, S]) for i in range(2)]
        raw_d = [at(f"raw_d{i}", 192 + 4 * i, [P, DT, KB]) for i in range(2)]
        raw_u = [at("raw_u0", 200, [P, MT, V]), at("raw_u1", 144, [P, MT, V])]
        ident = at("ident", 206, [P, P])
        sm = at("sm", 206.5, [P, 224])
        NB_BIAS = 2 * HT + 3 * DT
        bias = sm[:, 0:NB_BIAS]
        bp, cb1 = bias[:, 0:DT], bias[:, DT:DT + HT]
        cb2 = bias[:, DT + HT:2 * DT + HT]
        mb1 = bias[:, 2 * DT + HT:2 * DT + 2 * HT]
        mb2 = bias[:, 2 * DT + 2 * HT:3 * DT + 2 * HT]
        cbias = sm[:, 44:60].rearrange("p (b d) -> p b d", b=B)
        codes_f = sm[:, 60:64]
        feat_f = sm[:, 64:68]
        rowmax = sm[:, 68:72]
        negmax = sm[:, 72:76]
        rowsum = sm[:, 76:80]
        rowinv = sm[:, 80:84]
        pp = sm[:, 84:124].rearrange("p (b n) -> p b n", b=B)
        stats = sm[:, 124:148].rearrange("p (t n) -> p t n", n=6)
        mv = sm[:, 148:164].rearrange("p (i t n) -> p i t n", i=2, n=2)
        rstd = sm[:, 164:172].rearrange("p (i t) -> p i t", i=2)
        nmr = sm[:, 172:180].rearrange("p (i t) -> p i t", i=2)
        mhalf = sm[:, 180:184]
        ve = sm[:, 184:192].rearrange("p (i t) -> p i t", i=2)
        codes_i = at("codes_i", 206.5 + 0.875, [P, B], I32)
        experts = at("experts", 206.5 + 0.875 + 1 / 32, [1, B], I32)
        feat_i = at("feat_i", 206.5 + 0.875 + 2 / 32, [P, DT], I32)

        psum = ctx.enter_context(nc.psum_tensor("psum", [P, BANKS, 512], F32))
        bank = [psum[:, i, :] for i in range(BANKS)]
        ACC = [bank[4 + d] for d in range(DT)]
        DOWN = [bank[0], bank[1]]
        UP = [bank[2 + i] for i in range(DT)]
        TR = [bank[6], bank[7]]
        ROWS = bank[0:DT]

        def f(ap):
            return ap.bitcast(F32)

        s_w = [sem(f"weight_{n}_landed") for n in ("v", "p", "q", "k")]
        s_x = sem("x_rows_landed")
        s_small = sem("small_inputs_landed")
        s_idx = sem("experts_landed")
        s_ident = sem("identity_ready")
        s_iota = sem("iota_ready")
        s_cast = sem("codes_and_iota_cast")
        s_cbias = sem("cms_bias_ready")
        s_wp = sem("wp_hi_ready")
        s_wpl = sem("wp_split")
        bank_full = sem("bank_full")
        act_done = sem("act_done")
        dve_done = sem("dve_done")
        s_rmax = sem("row_max_found")
        s_nmax = sem("neg_row_max_ready")
        s_rinv = sem("row_sum_inverted")
        s_raw = [sem(f"raw_tile_landed_{i}") for i in range(NSLOT)]
        w_slot_free = sem("weight_slot_free")
        up_full = sem("up_bank_full")
        w_hi_done = sem("weight_hi_done")
        w_lo_done = sem("weight_lo_done")
        w_lo_pool = sem("weight_lo_done_pool")
        gelu_done = sem("gelu_done")
        g_hi_done = sem("g_hi_done")
        g_lo_done = sem("g_lo_done")
        s_acc1 = sem("cms_accumulated")
        s_acc2 = sem("modifier_accumulated")
        cms_hi_done = sem("cms_hi_done")
        cms_lo_done = sem("cms_lo_done")
        cms_added = sem("cms_added")
        mod_added = sem("modifier_added")
        y0_done = sem("y0_done")
        t_rawd = [sem(f"raw_down_landed_{i}") for i in range(2)]
        t_rawu = [sem(f"raw_up_landed_{i}") for i in range(2)]
        t_pp = [sem(f"unit_columns_landed_{i}") for i in range(B)]
        t_bc = [sem(f"unit_rows_landed_{i}") for i in range(2)]
        t_bup0 = sem("first_up_bias_landed")
        t_rows_full = sem("y0_rows_full")
        t_res_done = sem("y0_residual_done")
        t_yhi = sem("y_hi_done")
        t_ylo = sem("y_lo_done")
        t_yf = sem("y_scaled")
        t_down = sem("down_full")
        t_hf = sem("h_gelu_done")
        t_hhi = sem("h_hi_done")
        t_hlo = sem("h_lo_done")
        t_wdhi = sem("wd_hi_done")
        t_wdlo = sem("wd_lo_done")
        t_wuhi = sem("wu_hi_done")
        t_wulo = sem("wu_lo_done")
        t_up = sem("up_full")
        t_z = sem("z_summed")
        t_bn = sem("z_stats_taken")
        t_mv = sem("mean_var_ready")
        t_ve = sem("var_eps_ready")
        t_rstd = sem("rstd_ready")
        t_nmr = sem("shift_ready")
        t_zn = sem("z_normalised")
        t_tr = sem("transposed_full")
        t_bsum = sem("beta_sum_ready")
        t_rmul = sem("row_scaled")
        t_res = sem("row_result_ready")
        s_half = sem("minus_half_ready")
        s_ident0 = sem("identity_cleared")
        s_out = sem("output_stored")

        J_WV, J_WQ, J_WK, J_X0, J_VP, J_G, J_U0, J_V0, J_S0 = (4 * i for i in range(9))
        J_LOOP = 36
        JX, JPT, JU, JPV, JV, JS = (J_LOOP + 4 * i for i in range(6))
        PER = 24
        J_PT3 = J_LOOP + 3 * PER
        J_PV3 = J_PT3 + DT
        J_END = J_PV3 + DT
        SLOTS0 = NSLOT
        GF0 = 2
        Y0 = DT

        def w_ready(t, b, q=0):
            return 30 * b + 4 * q + t - 1

        block = ctx.enter_context(nc.Block())

        @block.sync
        def _(sp):
            for i in range(4):
                sp.dma_start(w_raw4[:, i, :, :], wts[i]).then_inc(s_w[i], 16)
            sp.dma_start(xrows[:, :, :], xin[0]).then_inc(s_x, 16)
            sp.dma_start(bias, bias_in).then_inc(s_small, 16)
            sp.dma_start(codes_i[:, :], codes_in.to_broadcast([P, B])).then_inc(s_small, 16)
            sp.dma_start(experts[:, :], experts_in).then_inc(s_idx, 16)
            sp.wait_ge(s_idx, 16)
            ex = [sp.value_load(experts[0:1, b:b + 1], min_val=0, max_val=EXPERTS - 1)
                  for b in range(B)]
            sp.wait_ge(bank_full, J_X0 + DT)
            sp.dma_start(xrows[:, :, :], xin[1]).then_inc(s_x, 16)
            with sp.Fori(0, 2) as b:
                sp.wait_ge(bank_full, b * PER + JX + DT)
                sp.dma_start(xrows[:, :, :], xin[bass.ds(b + 2, 1)].rearrange("o p k n -> p (o k) n")).then_inc(s_x, 16)
            sp.wait_ge(bank_full, J_PT3 + DT)
            with sp.Fori(0, B) as b:
                with sp.Fori(0, HT // NSLOT) as q:
                    for j in range(NSLOT):
                        if j == 2:
                            sp.wait_ge(bank_full, J_END)
                        sp.wait_ge(up_full, b * (2 * HT) + q * NSLOT + (j + 1))
                        sp.dma_start(raw[j][:, 0:W1], mlp1[bass.ds(q * NSLOT + j, 1)].rearrange("o p n -> (o p) n")).then_inc(s_raw[j], 16)
                with sp.Fori(0, HT // NSLOT) as q:
                    for j in range(NSLOT):
                        sp.wait_ge(up_full, b * (2 * HT) + q * NSLOT + (HT + j + 1))
                        sp.dma_start(raw[j][:, 0:W2], mlp2[bass.ds(q * NSLOT + j, 1)].rearrange("o p n -> (o p) n")).then_inc(s_raw[j], 16)

            def unit_loads(u, layer, b, first=False):
                row = layer * EXPERTS + ex[b]
                if not first:
                    sp.wait_ge(t_wdlo, u - 1)
                sp.dma_start(raw_d[b % 2][:, :, :], wd_all[bass.ds(row, 1)].rearrange("o p k n -> p (o k) n")).then_inc(t_rawd[b % 2], 16)
                if not first:
                    sp.wait_ge(t_wulo, u - 1)
                sp.dma_start(raw_u[b % 2][:, :, :], wu_all[bass.ds(row, 1)].rearrange("o p k n -> p (o k) n")).then_inc(t_rawu[b % 2], 16)

            def unit_columns(u, layer, b):
                if u >= B:
                    sp.wait_ge(t_yf, (u - 4) * DT + DT)
                row = layer * EXPERTS + ex[b]
                sp.dma_start(pp[:, b, :], pp_all[bass.ds(row, 1)].rearrange("o p n -> (o p) n")).then_inc(t_pp[b], 16)

            def unit_rows(u, layer, b):
                if u >= 2:
                    sp.wait_ge(t_res, (u - 2) * DT + DT)
                row = layer * EXPERTS + ex[b]
                sp.dma_start(bc[b % 2][:, 0:2, :], gb_all[bass.ds(row, 1)].to_broadcast([P, 2, V])).then_inc(t_bc[b % 2], 16)
                if layer < LAYERS - 1:
                    sp.dma_start(bc[b % 2][:, 2, :], bup_all[bass.ds(row + EXPERTS, 1)].to_broadcast([P, V])).then_inc(t_bc[b % 2], 16)

            TOT = 2 * HT * B
            sp.wait_ge(w_lo_done, 30 * B)
            sp.wait_ge(w_slot_free, SLOTS0 + TOT - 2)
            unit_loads(0, 0, 0, first=True)
            unit_loads(1, 0, 1, first=True)
            for b in range(B):
                sp.dma_start(bup0[:, b, :], bup_all[bass.ds(ex[b], 1)].to_broadcast([P, V])).then_inc(t_bup0, 16)
                unit_columns(b, 0, b)
            unit_rows(0, 0, 0)
            unit_loads(2, 0, 2)
            sp.wait_ge(w_slot_free, SLOTS0 + TOT)
            unit_rows(1, 0, 1)
            unit_loads(3, 0, 3)
            for u in range(4, 14):
                if u < 12:
                    unit_loads(u, u // B, u % B)
                    unit_columns(u, u // B, u % B)
                unit_rows(u - 2, (u - 2) // B, (u - 2) % B)
            for u in range(8, 12):
                for i in range(DT):
                    sp.wait_ge(t_res, u * DT + i + 1)
                    sp.dma_start(out[u % B, :, i, :], res[:, u % B, i, :]).then_inc(s_out, 16)
            sp.wait_ge(s_out, 16 * B * DT)

        @block.tensor
        def _(pe):
            def mm3(ps, lw, rw, first, last):
                nc.tensor.matmul(ps, lw(0), rw(0), start=first, stop=False)
                nc.tensor.matmul(ps, lw(0), rw(1), start=False, stop=False)
                return nc.tensor.matmul(ps, lw(1), rw(0), start=False, stop=last)

            def bank_wait(n):
                pe.wait_ge(dve_done, n - (BANKS - 1))

            def transposes(n, const, src, wait=None):
                for d in range(DT):
                    if const + d >= BANKS:
                        bank_wait(n + d)
                    for i in range(DT):
                        if wait and d == 0:
                            wait(i)
                        ins = nc.tensor.transpose(bank[(const + d) % BANKS][:, i * P:(i + 1) * P],
                                                  src[:, i, d * P:(d + 1) * P], ident[:, :])
                    ins.then_inc(bank_full, 1)

            def product(n, const, lhs, rhs, ready_l, ready_r):
                for m in range(DT):
                    bank_wait(n + m)
                    for k in range(DT):
                        if m == 0:
                            if ready_l is not None:
                                pe.wait_ge(dve_done, ready_l + (k + 1))
                            if ready_r is not None:
                                pe.wait_ge(dve_done, ready_r + (k + 1))
                        ins = mm3(bank[(const + m) % BANKS],
                                  lambda e: lhs[:, e, k, m * P:(m + 1) * P], lambda e: rhs[:, e, k, :],
                                  k == 0, k == DT - 1)
                    ins.then_inc(bank_full, 1)

            pe.wait_ge(s_ident, 1)
            pe.wait_ge(s_w[0], 16)
            transposes(J_WV, J_WV, w_raw4[:, 0, :, :])
            pe.wait_ge(s_w[2], 16)
            transposes(J_WQ, J_WQ, w_raw4[:, 2, :, :])
            pe.wait_ge(s_w[3], 16)
            transposes(J_WK, J_WK, w_raw4[:, 3, :, :])
            pe.wait_ge(s_x, 16)
            transposes(J_X0, J_X0, xrows[:, :, :])
            pe.wait_ge(s_wpl, 1)
            product(J_VP, J_VP, wvT, wp_s, J_WV, None)
            product(J_G, J_G, wqT, wkT, J_WQ, J_WK)
            product(J_U0, J_U0, g_w, xT, J_G, J_X0)
            product(J_V0, J_V0, xT, vp_w, None, J_VP)
            product(J_S0, J_S0, uT, xT, J_U0, None)
            with pe.Fori(0, B - 1) as b:
                n = b * PER
                pe.wait_ge(s_x, b * 16 + 32)
                transposes(n + JX, JX, xrows[:, :, :])
                pe.wait_ge(dve_done, n + JX)
                transposes(n + JPT, JPT, probs[:, :, :])
                product(n + JU, JU, g_w, xT, None, n + JX)
                product(n + JPV, JPV, v_n, pT, None, n + JPT)
                product(n + JV, JV, xT, vp_w, None, None)
                product(n + JS, JS, uT, xT, n + JU, None)
            pe.wait_ge(dve_done, J_PT3)
            for d in range(DT):
                bank_wait(J_PT3 + d)
                for i in range(DT):
                    ins = nc.tensor.transpose(bank[(J_PT3 + d) % BANKS][:, i * P:(i + 1) * P],
                                              probs[:, i, d * P:(d + 1) * P], ident[:, :])
                    if d == DT - 1 and i == 0:
                        ins.then_inc(w_slot_free, SLOTS0)
                    if d == DT - 1 and i == 1:
                        ins.then_inc(up_full, SLOTS0)
                    if d == DT - 1 and i == 2:
                        ins.then_inc(y0_done, Y0)
                    if d == DT - 2 and i == 0:
                        ins.then_inc(g_lo_done, GF0)
                ins.then_inc(bank_full, 1)
            product(J_PV3, J_PV3, v_n, pT, None, J_PT3)
            pe.wait_ge(dve_done, J_END)

            with pe.Fori(0, B) as b:
                def up_a(t, width, first, last):
                    s = t % NSLOT
                    for k in range(DT):
                        ins = mm3(bank[s], lambda e: w_hl[s][:, e, k * P:(k + 1) * P],
                                  lambda e: a_all[:, bass.ds(b, 1), e, k, :].rearrange("p o n -> p (o n)"),
                                  first and k == 0, last and k == DT - 1)
                    return ins

                def up_c(t, wait=False):
                    s = t % NSLOT
                    for k in range(DT):
                        if wait:
                            pe.wait_ge(cms_lo_done, b * DT + (k + 1))
                        ins = mm3(bank[s], lambda e: w_hl[s][:, e, (DT + k) * P:(DT + k + 1) * P],
                                  lambda e: cms[:, e, k, :], False, k == DT - 1)
                    return ins

                def down(t, q, off, first=False, last=False, done=None):
                    s = t % NSLOT
                    pe.wait_ge(g_lo_done, b * (2 * HT) + q * NSLOT + (GF0 + t + 1))
                    for d in range(DT):
                        ins = mm3(ACC[d], lambda e: w_hl[s][:, e, off + d * P:off + (d + 1) * P],
                                  lambda e: g_hl[s][:, e, :], first, last)
                        if done is not None and d < DT - 1:
                            ins.then_inc(done, 1)
                        elif done is not None:
                            ins.then_inc(done, 1)
                    return ins

                def down_free(t, q, off, **kw):
                    down(t, q, off, **kw).then_inc(w_slot_free, 1)

                D1, D2 = DT * P, 2 * DT * P
                pe.wait_ge(w_lo_pool, b * 2 + 1)
                up_a(0, W1, True, True).then_inc(up_full, 1)
                pe.wait_ge(w_lo_pool, b * 2 + 2)
                up_a(1, W1, True, True).then_inc(up_full, 1)
                pe.wait_ge(w_lo_done, w_ready(2, b))
                up_a(2, W1, True, True).then_inc(up_full, 1)
                pe.wait_ge(y0_done, b * DT + Y0)
                down_free(0, 0, D1, first=True)
                pe.wait_ge(w_lo_done, w_ready(3, b))
                up_a(3, W1, True, True).then_inc(up_full, 1)
                down_free(1, 0, D1)
                with pe.Fori(0, HT // NSLOT - 1) as q:
                    for j in range(NSLOT):
                        pe.wait_ge(w_lo_done, w_ready(4 + j, b, q))
                        up_a(4 + j, W1, True, True).then_inc(up_full, 1)
                        down_free(2 + j, q, D1)
                pe.wait_ge(w_lo_done, w_ready(16, b))
                up_a(16, W2, True, False)
                down_free(14, 0, D1)
                pe.wait_ge(w_lo_done, w_ready(17, b))
                up_a(17, W2, True, False)
                down(15, 0, D1, last=True).then_inc(w_slot_free, 1)
                pe.wait_ge(w_lo_done, w_ready(18, b))
                up_a(18, W2, True, False)
                up_c(16, wait=True).then_inc(up_full, 1)
                up_c(17).then_inc(up_full, 1)
                up_c(18).then_inc(up_full, 1)
                pe.wait_ge(cms_added, (b + 1) * DT)
                down_free(16, 0, D2, first=True)
                pe.wait_ge(w_lo_done, w_ready(19, b))
                up_a(19, W2, True, False)
                up_c(19).then_inc(up_full, 1)
                down_free(17, 0, D2)
                with pe.Fori(0, HT // NSLOT - 1) as q:
                    for j in range(NSLOT):
                        pe.wait_ge(w_lo_done, w_ready(20 + j, b, q))
                        up_a(20 + j, W2, True, False)
                        up_c(20 + j).then_inc(up_full, 1)
                        down_free(18 + j, q, D2)
                down_free(30, 0, D2)
                down_free(31, 0, D2, last=True)

            for b in range(B):
                pe.wait_ge(y0_done, Y0 + (b + 1) * DT)
                for i in range(DT):
                    if b:
                        pe.wait_ge(t_res_done, (b - 1) * DT + i + 1)
                    for d in range(DT):
                        ins = nc.tensor.transpose(ROWS[i][:, d * P:(d + 1) * P],
                                                  res[:, b, d, i * P:(i + 1) * P], ident[:, :])
                    ins.then_inc(t_rows_full, 1)

            def t_down_mm(u, b):
                pe.wait_ge(t_wdlo, u + 1)
                for m in range(MT):
                    if u > 0:
                        pe.wait_ge(t_hf, (u - 1) * MT + m + 1)
                    else:
                        pe.wait_ge(t_res_done, (B - 1) * DT + m + 1)
                    for k in range(DT):
                        if m == 0:
                            pe.wait_ge(t_ylo, u * DT + (k + 1))
                        ins = mm3(DOWN[m], lambda e: wd[b % 2][:, e, k, m * P:(m + 1) * P],
                                  lambda e: yT[b][:, e, k, :], k == 0, k == DT - 1)
                    ins.then_inc(t_down, 1)

            def t_up_mm(u, b):
                pe.wait_ge(t_wulo, u + 1)
                for i in range(DT):
                    if isinstance(u, int) and u == 0:
                        pe.wait_ge(t_res_done, B * DT)
                    else:
                        pe.wait_ge(t_z, u * DT - DT + i + 1)
                    for k in range(MT):
                        if i == 0:
                            pe.wait_ge(t_hlo, u * MT + (k + 1))
                        ins = mm3(UP[i], lambda e: h_hl[b % 2][:, e, k, i * P:(i + 1) * P],
                                  lambda e: wu[b % 2][:, e, k, :], k == 0, k == MT - 1)
                    ins.then_inc(t_up, 1)

            def t_transpose(u, b):
                for d in range(DT):
                    if isinstance(u, int) and u * DT + d < 2:
                        pass
                    else:
                        pe.wait_ge(t_yf, u * DT + (d - 1))
                    for i in range(DT):
                        if d == 0:
                            pe.wait_ge(t_zn, u * DT + (i + 1))
                        ins = nc.tensor.transpose(TR[d % 2][:, i * P:(i + 1) * P],
                                                  z[b % 2][:, i, d * P:(d + 1) * P], ident[:, :])
                    ins.then_inc(t_tr, 1)

            for s in range(13):
                if s < 12:
                    t_down_mm(s, s % B)
                if 1 <= s:
                    t_up_mm(s - 1, (s - 1) % B)
                if 2 <= s < 10:
                    t_transpose(s - 2, (s - 2) % B)

        @block.scalar
        def _(act):
            def hi_jobs(n, const, dst, keep=None, scale=None):
                for m in range(DT):
                    act.wait_ge(bank_full, n + (m + 1))
                    src = bank[(const + m) % BANKS]
                    if keep is not None:
                        nc.scalar.copy(keep(m), src)
                    if scale is None:
                        nc.scalar.copy(dst(m), src).then_inc(act_done, 1)
                    else:
                        nc.scalar.activation(dst(m), src, ACT.Identity, scale=scale).then_inc(act_done, 1)

            def exp_jobs(n, const):
                for m in range(DT):
                    act.wait_ge(s_nmax, n_s(n, m))
                    nc.scalar.activation(probs[:, m, :], bank[(const + m) % BANKS], ACT.Exp,
                                         bias=negmax[:, m:m + 1], accum_out=rowsum[:, m:m + 1]).then_inc(act_done, 1)

            def n_s(seq, m):
                return seq * DT + (m + 1)

            hi_jobs(J_WV, J_WV, lambda m: wvT[:, 0, m, :])
            act.wait_ge(s_w[1], 16)
            nc.scalar.copy(wp_s[:, 0, :, :], w_raw4[:, 1, :, :]).then_inc(s_wp, 1)
            hi_jobs(J_WQ, J_WQ, lambda m: wqT[:, 0, m, :])
            hi_jobs(J_WK, J_WK, lambda m: wkT[:, 0, m, :])
            hi_jobs(J_X0, J_X0, lambda m: xT[:, 0, m, :], keep=lambda m: res[:, 0, m, :])
            hi_jobs(J_VP, J_VP, lambda m: vp_w[:, 0, m, :])
            hi_jobs(J_G, J_G, lambda m: g_w[:, 0, m, :])
            hi_jobs(J_U0, J_U0, lambda m: uT[:, 0, m, :], scale=SCALE)
            hi_jobs(J_V0, J_V0, lambda m: v_n[:, 0, m, :])
            exp_jobs(0, J_S0)

            act.wait_ge(s_small, 32)

            def attn_jobs(n, const, b):
                for m in range(DT):
                    act.wait_ge(bank_full, n + (m + 1))
                    dst = (a_all[:, b, 0, m, :] if isinstance(b, int) else
                           a_all[:, bass.ds(b, 1), 0, m, :].rearrange("p o n -> p (o n)"))
                    nc.scalar.activation(dst, bank[(const + m) % BANKS], ACT.Identity,
                                         bias=bp[:, m:m + 1]).then_inc(act_done, 1)

            with act.Fori(0, B - 1) as b:
                n = b * PER
                hi_jobs(n + JX, JX, lambda m: xT[:, 0, m, :],
                        keep=lambda m: res[:, bass.ds(b + 1, 1), m, :].rearrange("p o n -> p (o n)"))
                hi_jobs(n + JPT, JPT, lambda m: pT[:, 0, m, :])
                hi_jobs(n + JU, JU, lambda m: uT[:, 0, m, :], scale=SCALE)
                attn_jobs(n + JPV, JPV, b)
                hi_jobs(n + JV, JV, lambda m: v_n[:, 0, m, :])
                exp_jobs(b + 1, JS)
            hi_jobs(J_PT3, J_PT3, lambda m: pT[:, 0, m, :])
            attn_jobs(J_PV3, J_PV3, B - 1)

            with act.Fori(0, B) as b:
                def gelu(t, q, bias_ap):
                    s = t % NSLOT
                    act.wait_ge(up_full, b * (2 * HT) + q * NSLOT + (SLOTS0 + t + 1))
                    act.wait_ge(g_lo_done, b * (2 * HT) + q * NSLOT + (GF0 + t - 1))
                    nc.scalar.activation(gf[t % 2][:, :], bank[s], ACT.Gelu, bias=bias_ap).then_inc(gelu_done, 1)
                    act.wait_ge(gelu_done, b * (2 * HT) + q * NSLOT + (t + 1))
                    nc.scalar.copy(g_hl[s][:, 0, :], gf[t % 2][:, :]).then_inc(g_hi_done, 1)

                def w_hi(t, q, width, n):
                    s = t % NSLOT
                    act.wait_ge(s_raw[s], (b * (2 * HT // NSLOT) + q + (n + 1)) * 16)
                    act.wait_ge(w_slot_free, b * (2 * HT) + q * NSLOT + (t + 1))
                    nc.scalar.copy(w_hl[s][:, 0, 0:width], raw[s][:, 0:width]).then_inc(w_hi_done, 1)

                w_hi(0, 0, W1, 0)
                w_hi(1, 0, W1, 0)
                with act.Fori(0, HT // NSLOT - 1) as q:
                    for j in range(NSLOT):
                        gelu(j, q, cb1[:, bass.ds(q * NSLOT + j, 1)])
                        w_hi(j + 2, q, W1, (j + 2) // NSLOT)
                for t in range(12, 16):
                    gelu(t, 0, cb1[:, t:t + 1])
                    w_hi(t + 2, 0, W1 if t + 2 < HT else W2, (t + 2) // NSLOT)
                w_hi(18, 0, W2, 4)
                for d in range(DT):
                    act.wait_ge(w_slot_free, b * (2 * HT) + (SLOTS0 + HT))
                    nc.scalar.activation(cms[:, 0, d, :], ACC[d], ACT.Identity,
                                         bias=cbias[:, bass.ds(b, 1), d]).then_inc(cms_hi_done, 1)
                with act.Fori(0, HT // NSLOT - 1) as q:
                    for j in range(NSLOT):
                        gelu(HT + j, q, mb1[:, bass.ds(q * NSLOT + j, 1)])
                        w_hi(HT + j + 3, q, W2, (HT + j + 3) // NSLOT)
                for t in range(28, 32):
                    gelu(t, 0, mb1[:, t - HT:t - HT + 1])
                    if t + 3 < 32:
                        w_hi(t + 3, 0, W2, (t + 3) // NSLOT)

            TOT = 2 * HT * B
            act.wait_ge(w_slot_free, SLOTS0 + TOT - 2)

            def wd_hi(u):
                act.wait_ge(t_rawd[u % 2], 16 * (u // 2 + 1))
                if u >= 2:
                    act.wait_ge(t_down, (u - 1) * MT)
                nc.scalar.copy(wd[u % 2][:, 0, :, :], raw_d[u % 2][:, :, :]).then_inc(t_wdhi, 1)

            def wu_hi(u):
                act.wait_ge(t_rawu[u % 2], 16 * (u // 2 + 1))
                if u >= 2:
                    act.wait_ge(t_up, (u - 1) * DT)
                nc.scalar.copy(wu[u % 2][:, 0, :, :], raw_u[u % 2][:, :, :]).then_inc(t_wuhi, 1)

            def y0_hi(b):
                act.wait_ge(y0_done, Y0 + (b + 1) * DT)
                for d in range(DT):
                    nc.scalar.copy(yT[b][:, 0, d, :], res[:, b, d, :]).then_inc(t_yhi, 1)

            wd_hi(0)
            act.wait_ge(up_full, SLOTS0 + TOT)
            y0_hi(0)
            act.wait_ge(w_slot_free, SLOTS0 + TOT)
            wu_hi(0)
            for b in range(1, B):
                y0_hi(b)
            for s in range(14):
                if 2 <= s:
                    u = s - 2
                    for i in range(DT):
                        act.wait_ge(t_nmr, u + 1)
                        nc.scalar.activation(z[u % 2][:, i, :], z[u % 2][:, i, :], ACT.Identity,
                                             scale=rstd[:, u % 2, i:i + 1], bias=nmr[:, u % 2, i:i + 1]).then_inc(t_zn, 1)
                if s < 12:
                    for m in range(MT):
                        act.wait_ge(t_down, s * MT + m + 1)
                        if m == 0:
                            act.wait_ge(t_pp[s % B], 16 * (s // B + 1))
                        if s > 0:
                            act.wait_ge(t_hlo, (s - 1) * MT + m + 1)
                        nc.scalar.activation(hf[m][:, :], DOWN[m], ACT.Gelu, bias=pp[:, s % B, 8 + m:9 + m]).then_inc(t_hf, 1)
                        act.wait_ge(t_hf, s * MT + m + 1)
                        if s >= 2:
                            act.wait_ge(t_up, (s - 1) * DT)
                        nc.scalar.copy(h_hl[s % 2][:, 0, m, :], hf[m][:, :]).then_inc(t_hhi, 1)
                    if s + 1 < 12:
                        wd_hi(s + 1)
                    if s >= 1:
                        wu_hi(s)
                if 2 <= s < 10:
                    u = s - 2
                    for d in range(DT):
                        n = u * DT + d
                        act.wait_ge(t_tr, n + 1)
                        act.wait_ge(t_ylo, B * DT + n - 1)
                        nc.scalar.activation(yf[d % 2][:, :], TR[d % 2], ACT.Identity,
                                             scale=pp[:, u % B, d:d + 1], bias=pp[:, u % B, 4 + d:5 + d]).then_inc(t_yf, 1)
                        act.wait_ge(t_yf, n + 1)
                        nc.scalar.copy(yT[u % B][:, 0, d, :], yf[d % 2][:, :]).then_inc(t_yhi, 1)

        @block.vector
        def _(dve):
            def lo_jobs(n, const, tile, scale=None):
                for m in range(DT):
                    dve.wait_ge(act_done, n + (m + 1))
                    src = bank[(const + m) % BANKS]
                    if scale is None:
                        nc.vector.tensor_tensor(tile[:, 1, m, :], src, f(tile[:, 0, m, :]), ALU.subtract).then_inc(dve_done, 1)
                    else:
                        nc.vector.scalar_tensor_tensor(out=tile[:, 1, m, :], in0=src, scalar=scale, in1=f(tile[:, 0, m, :]),
                                                       op0=ALU.mult, op1=ALU.subtract).then_inc(dve_done, 1)

            def softmax_jobs(n, const, seq):
                for m in range(DT):
                    dve.wait_ge(bank_full, n + (m + 1))
                    nc.vector.reduce_max(rowmax[:, m:m + 1], bank[(const + m) % BANKS], AX.X).then_inc(s_rmax, 1)
                    dve.wait_ge(s_rmax, seq * DT + (m + 1))
                    nc.vector.tensor_scalar(negmax[:, m:m + 1], rowmax[:, m:m + 1], -1.0, None, ALU.mult).then_inc(s_nmax, 1)
                for m in range(DT):
                    dve.wait_ge(act_done, n + (m + 1))
                    nc.vector.reciprocal(rowinv[:, m:m + 1], rowsum[:, m:m + 1]).then_inc(s_rinv, 1)
                    dve.wait_ge(s_rinv, seq * DT + (m + 1))
                    nc.vector.tensor_scalar(probs[:, m, :], probs[:, m, :], rowinv[:, m:m + 1], None, ALU.mult).then_inc(dve_done, 1)

            def attn_lo(n, const, b):
                for m in range(DT):
                    dve.wait_ge(act_done, n + (m + 1))
                    hi, lo = ((a_all[:, b, e, m, :] if isinstance(b, int) else
                               a_all[:, bass.ds(b, 1), e, m, :].rearrange("p o n -> p (o n)")) for e in range(2))
                    nc.vector.scalar_tensor_tensor(out=lo, in0=bank[(const + m) % BANKS], scalar=bp[:, m:m + 1], in1=f(hi),
                                                   op0=ALU.add, op1=ALU.subtract).then_inc(dve_done, 1)

            lo_jobs(J_WV, J_WV, wvT)
            dve.wait_ge(s_wp, 1)
            nc.vector.tensor_tensor(wp_s[:, 1, :, :], w_raw4[:, 1, :, :], f(wp_s[:, 0, :, :]), ALU.subtract).then_inc(s_wpl, 1)
            lo_jobs(J_WQ, J_WQ, wqT)
            lo_jobs(J_WK, J_WK, wkT)
            lo_jobs(J_X0, J_X0, xT)
            dve.wait_ge(s_small, 32)
            dve.wait_ge(s_iota, 1)
            nc.vector.tensor_copy(codes_f, codes_i[:, :]).then_inc(s_cast, 1)
            nc.vector.tensor_copy(feat_f, feat_i[:, :]).then_inc(s_cast, 1)
            dve.wait_ge(s_cast, 2)
            for b in range(B):
                nc.vector.scalar_tensor_tensor(out=cbias[:, b, :], in0=feat_f, scalar=codes_f[:, b:b + 1], in1=cb2,
                                               op0=ALU.is_equal, op1=ALU.add).then_inc(s_cbias, 1)
            lo_jobs(J_VP, J_VP, vp_w)
            lo_jobs(J_G, J_G, g_w)
            lo_jobs(J_U0, J_U0, uT, scale=SCALE)
            lo_jobs(J_V0, J_V0, v_n)
            softmax_jobs(J_S0, J_S0, 0)
            with dve.Fori(0, B - 1) as b:
                n = b * PER
                lo_jobs(n + JX, JX, xT)
                lo_jobs(n + JPT, JPT, pT)
                lo_jobs(n + JU, JU, uT, scale=SCALE)
                attn_lo(n + JPV, JPV, b)
                lo_jobs(n + JV, JV, v_n)
                softmax_jobs(n + JS, JS, b + 1)
            lo_jobs(J_PT3, J_PT3, pT)
            attn_lo(J_PV3, J_PV3, B - 1)

            with dve.Fori(0, B) as b:
                def seq_res(d):
                    return res[:, bass.ds(b, 1), d, :].rearrange("p o n -> p (o n)")

                def g_lo(t, q):
                    s = t % NSLOT
                    dve.wait_ge(g_hi_done, b * (2 * HT) + q * NSLOT + (t + 1))
                    nc.vector.tensor_tensor(g_hl[s][:, 1, :], gf[t % 2][:, :], f(g_hl[s][:, 0, :]), ALU.subtract).then_inc(g_lo_done, 1)

                def w_lo(t, q, width):
                    s = t % NSLOT
                    dve.wait_ge(w_hi_done, b * (2 * HT) + q * NSLOT + (t + 1))
                    nc.vector.tensor_tensor(w_hl[s][:, 1, 0:width], raw[s][:, 0:width], f(w_hl[s][:, 0, 0:width]), ALU.subtract).then_inc(w_lo_done, 1)

                with dve.Fori(0, HT // NSLOT - 1) as q:
                    for j in range(NSLOT):
                        g_lo(j, q)
                        w_lo(j + 2, q, W1)
                for t in range(12, 16):
                    g_lo(t, 0)
                    w_lo(t + 2, 0, W1 if t + 2 < HT else W2)
                w_lo(18, 0, W2)
                for d in range(DT):
                    dve.wait_ge(cms_hi_done, b * DT + (d + 1))
                    nc.vector.scalar_tensor_tensor(out=cms[:, 1, d, :], in0=ACC[d], scalar=cbias[:, bass.ds(b, 1), d],
                                                   in1=f(cms[:, 0, d, :]), op0=ALU.add, op1=ALU.subtract).then_inc(cms_lo_done, 1)
                for d in range(DT):
                    nc.vector.scalar_tensor_tensor(out=seq_res(d), in0=ACC[d], scalar=cbias[:, bass.ds(b, 1), d],
                                                   in1=seq_res(d), op0=ALU.add, op1=ALU.add).then_inc(cms_added, 1)
                with dve.Fori(0, HT // NSLOT - 1) as q:
                    for j in range(NSLOT):
                        g_lo(HT + j, q)
                        w_lo(HT + j + 3, q, W2)
                for t in range(28, 32):
                    g_lo(t, 0)
                    if t + 3 < 32:
                        w_lo(t + 3, 0, W2)
                for d in range(DT):
                    dve.wait_ge(w_slot_free, b * (2 * HT) + (SLOTS0 + 2 * HT))
                    nc.vector.scalar_tensor_tensor(out=seq_res(d), in0=ACC[d], scalar=mb2[:, d:d + 1],
                                                   in1=seq_res(d), op0=ALU.add, op1=ALU.add).then_inc(mod_added, 1)
                for d in range(DT):
                    dve.wait_ge(mod_added, b * DT + (d + 1))
                    nc.vector.tensor_scalar(seq_res(d), seq_res(d), 0.0, 1.0, ALU.max, ALU.min).then_inc(y0_done, 1)

            def wd_lo(u):
                dve.wait_ge(t_wdhi, u + 1)
                nc.vector.tensor_tensor(wd[u % 2][:, 1, :, :], raw_d[u % 2][:, :, :], f(wd[u % 2][:, 0, :, :]), ALU.subtract).then_inc(t_wdlo, 1)

            def wu_lo(u):
                dve.wait_ge(t_wuhi, u + 1)
                nc.vector.tensor_tensor(wu[u % 2][:, 1, :, :], raw_u[u % 2][:, :, :], f(wu[u % 2][:, 0, :, :]), ALU.subtract).then_inc(t_wulo, 1)

            def y0_lo(b):
                for d in range(DT):
                    dve.wait_ge(t_yhi, b * DT + d + 1)
                    nc.vector.tensor_tensor(yT[b][:, 1, d, :], res[:, b, d, :], f(yT[b][:, 0, d, :]), ALU.subtract).then_inc(t_ylo, 1)

            def y0_rows(b):
                dve.wait_ge(t_ylo, (b + 1) * DT)
                for i in range(DT):
                    dve.wait_ge(t_rows_full, (b + 1) * DT)
                    dve.wait_ge(t_bup0, 16 * B)
                    nc.vector.tensor_tensor(res[:, b, i, :], ROWS[i], bup0[:, b, :], ALU.add).then_inc(t_res_done, 1)

            wd_lo(0)
            y0_lo(0)
            y0_rows(0)
            wu_lo(0)
            for b in range(1, B):
                y0_lo(b)
                y0_rows(b)
            for s in range(14):
                if 2 <= s:
                    u = s - 2
                    dve.wait_ge(t_rstd, u + 1)
                    nc.vector.scalar_tensor_tensor(out=nmr[:, u % 2, :], in0=mv[:, u % 2, :, 0], scalar=-1.0, in1=rstd[:, u % 2, :],
                                                   op0=ALU.mult, op1=ALU.mult).then_inc(t_nmr, 1)
                if s < 12:
                    for m in range(MT):
                        dve.wait_ge(t_hhi, s * MT + m + 1)
                        nc.vector.tensor_tensor(h_hl[s % 2][:, 1, m, :], hf[m][:, :], f(h_hl[s % 2][:, 0, m, :]), ALU.subtract).then_inc(t_hlo, 1)
                    if s + 1 < 12:
                        wd_lo(s + 1)
                    if s >= 1:
                        wu_lo(s)
                if 1 <= s < 13:
                    u = s - 1
                    for i in range(DT):
                        dve.wait_ge(t_up, u * DT + i + 1)
                        if u >= B:
                            dve.wait_ge(t_res, (u - B) * DT + i + 1)
                        if u >= 2:
                            dve.wait_ge(t_rmul, (u - 2) * DT + i + 1)
                            dve.wait_ge(t_tr, min((u - 1) * DT, 8 * DT))
                        nc.vector.tensor_tensor(z[u % 2][:, i, :], UP[i], res[:, u % B, i, :], ALU.add).then_inc(t_z, 1)
                        dve.wait_ge(t_z, u * DT + i + 1)
                        nc.vector.bn_stats(stats[:, i, :], z[u % 2][:, i, :]).then_inc(t_bn, 1)
                        dve.wait_ge(t_bn, u * DT + i + 1)
                        if i == 0 and u >= 2:
                            dve.wait_ge(t_nmr, u - 1)
                        nc.vector.bn_aggr(mv[:, u % 2, i, :], stats[:, i, :]).then_inc(t_mv, 1)
                if 2 <= s < 10:
                    u = s - 2
                    for d in range(DT):
                        n = (u + B) * DT + d
                        dve.wait_ge(t_yhi, n + 1)
                        nc.vector.tensor_tensor(yT[u % B][:, 1, d, :], yf[d % 2][:, :], f(yT[u % B][:, 0, d, :]), ALU.subtract).then_inc(t_ylo, 1)

        @block.gpsimd
        def _(pool):
            nc.gpsimd.memset(ident[:, :], 0.0).then_inc(s_ident0, 1)
            pool.wait_ge(s_ident0, 1)
            nc.gpsimd.affine_select(out=ident[:, :], in_=ident[:, :], compare_op=ALU.not_equal, fill=1.0, base=0,
                                    pattern=[[-1, P]], channel_multiplier=1).then_inc(s_ident, 1)
            nc.gpsimd.iota(feat_i[:, :], pattern=[[P, DT]], base=0, channel_multiplier=1).then_inc(s_iota, 1)
            nc.gpsimd.memset(mhalf, -0.5).then_inc(s_half, 1)

            with pool.Fori(0, B) as b:
                for t in range(2):
                    pool.wait_ge(w_hi_done, b * (2 * HT) + (t + 1))
                    nc.gpsimd.tensor_tensor(w_hl[t][:, 1, 0:W1], raw[t][:, 0:W1], f(w_hl[t][:, 0, 0:W1]), ALU.subtract).then_inc(w_lo_pool, 1)

            pool.wait_ge(s_half, 1)
            for u in range(12):
                i2 = u % 2
                pool.wait_ge(t_mv, (u + 1) * DT)
                if u >= 2:
                    pool.wait_ge(t_zn, (u - 1) * DT)
                nc.gpsimd.tensor_scalar(ve[:, i2, :], mv[:, i2, :, 1], EPS, 1.0, ALU.add, ALU.mult).then_inc(t_ve, 1)
                pool.wait_ge(t_ve, u + 1)
                nc.gpsimd.tensor_tensor(rstd[:, i2, :], ve[:, i2, :], mhalf, ALU.pow).then_inc(t_rstd, 1)
                loads = sum(2 if v < 8 else 1 for v in range(i2, u + 1, 2))
                pool.wait_ge(t_bc[i2], 16 * loads)
                if u < 8:
                    nc.gpsimd.tensor_tensor(bc[i2][:, 3, :], bc[i2][:, 1, :], bc[i2][:, 2, :], ALU.add).then_inc(t_bsum, 1)
                for i in range(DT):
                    pool.wait_ge(t_zn, u * DT + i + 1)
                    if i == 0 and u < 8:
                        pool.wait_ge(t_bsum, u + 1)
                    nc.gpsimd.tensor_tensor(res[:, u % B, i, :], z[i2][:, i, :], bc[i2][:, 0, :], ALU.mult).then_inc(t_rmul, 1)
                    pool.wait_ge(t_rmul, u * DT + i + 1)
                    nc.gpsimd.tensor_tensor(res[:, u % B, i, :], res[:, u % B, i, :], bc[i2][:, 3 if u < 8 else 1, :], ALU.add).then_inc(t_res, 1)


_OUT = "out_dram"


def kernel(**inputs):
    import numpy as np
    import concourse.bacc as bacc
    from concourse.bass_utils import run_bass_kernel_spmd

    a = {k: np.asarray(v) for k, v in inputs.items()}

    def rows(w):
        return np.ascontiguousarray(w.reshape(-1, P, w.shape[-1]).transpose(1, 0, 2))

    def cols(v):
        return v.reshape(-1, P).T

    def up_tiles(w):
        k, t = w.shape[0] // P, w.shape[1] // P
        return w.reshape(k, P, t, P).transpose(2, 1, 0, 3).reshape(t, P, k * P)

    wts = np.stack([rows(a["L0_cond_" + n]) for n in ("Wv", "Wp", "Wq", "Wk")])
    mlp1 = np.concatenate([up_tiles(a["L0_cond_cW1"]), a["L0_cond_cW2"].reshape(HT, P, V)], axis=2)
    mlp2 = np.concatenate([up_tiles(a["L0_cond_mW1"]), a["L0_cond_mW2"].reshape(HT, P, V)], axis=2)
    bias = np.concatenate([cols(a["L0_cond_" + n]) for n in ("bp", "cb1", "cb2", "mb1", "mb2")], axis=1)
    names = [("L1", "ln_w", "ln_b"), ("L2", "gamma", "beta"), ("L3", "gamma", "beta")]
    wd, wu, pp, gb, bup = [], [], [], [], []
    for l, g, bt in names:
        for e in range(EXPERTS):
            wd.append(rows(a[f"{l}_cond_W_down"][e]))
            wu.append(rows(a[f"{l}_cond_W_up"][e]))
            pp.append(np.concatenate([cols(a[f"{l}_cond_{g}"][e]), cols(a[f"{l}_cond_{bt}"][e]),
                                      cols(a[f"{l}_cond_b_down"][e])], axis=1))
            gb.append(np.stack([a[f"{l}_cond_{g}"][e], a[f"{l}_cond_{bt}"][e]]))
            bup.append(a[f"{l}_cond_b_up"][e])
    arrays = {
        "wts": wts, "x": np.stack([rows(a["x"][b]) for b in range(B)]), "bias": bias,
        "codes": a["itok_B_17_1546"].reshape(1, B), "experts": a["itok_B_1_2"].reshape(1, B),
        "mlp1": mlp1, "mlp2": mlp2, "wd": np.stack(wd), "wu": np.stack(wu), "pp": np.stack(pp),
        "gb": np.stack(gb), "bup": np.stack(bup),
    }
    arrays = {k + "_dram": np.ascontiguousarray(v) for k, v in arrays.items()}
    nc = bacc.Bacc("TRN2", target_bir_lowering=False, num_devices=1)
    args = [nc.dram_tensor(k, v.shape, mybir.dt.from_np(v.dtype), kind="ExternalInput").ap()
            for k, v in arrays.items()]
    args.append(nc.dram_tensor(_OUT, (B, P, DT, V), F32, kind="ExternalOutput").ap())
    build(nc, *args)
    r = run_bass_kernel_spmd(nc, [arrays], core_ids=[0])
    got = r.results[0][_OUT]
    return np.ascontiguousarray(got.transpose(0, 2, 1, 3)).reshape(B, S, V)
```

```python
from contextlib import ExitStack

import concourse.bass as bass
from concourse import mybir

F32 = mybir.dt.float32
F32R = mybir.dt.float32r
I32 = mybir.dt.int32
ALU = mybir.AluOpType
ACT = mybir.ActivationFunctionType
AX = mybir.AxisListType

P = 128
B = 4
S = 512
V = 512
H = 4 * V
KB = 256
LAYERS = 3
EXPERTS = 3
DT = V // P
MT = KB // P
HT = H // P
SCALE = V ** -0.5
EPS = 1e-5
W1 = DT * P + V
W2 = 2 * DT * P + V
NSLOT = 4
PC = 512
NPC = (DT * KB + MT * V) // PC
NPIECE = LAYERS * EXPERTS * NPC
PHASE = NPIECE // B
PSLOT = 3
BANKS = 8
KiB = 1024


def build(nc, wts, xin, bias_in, codes_in, experts_in, mlp1, mlp2, wdu_all, pp_all, gb_all,
          bup_all, out):
    ctx = ExitStack()
    with ctx:
        base = -(-nc.sbuf_base // 64) * 64

        def at(name, kib, shape, dt=F32):
            return nc.alloc_sbuf_tensor_at(name, shape, dt, offset=base + int(kib * KiB))

        def sem(name):
            return ctx.enter_context(nc.semaphore(name))

        a_all = at("a_all", 0, [P, B, 2, DT, S], F32R)
        wqT = at("wqT", 0, [P, 2, DT, V], F32R)
        wkT = at("wkT", 16, [P, 2, DT, V], F32R)
        wvT = at("wvT", 32, [P, 2, DT, V], F32R)
        xrows = at("xrows", 48, [P, DT, V])
        g_w = at("g_w", 64, [P, 2, DT, V], F32R)
        vp_w = at("vp_w", 80, [P, 2, DT, V], F32R)
        xT = at("xT", 96, [P, 2, DT, S], F32R)
        uT = at("uT", 112, [P, 2, DT, S], F32R)
        v_n = at("v_n", 128, [P, 2, DT, V], F32R)
        pT = at("pT", 144, [P, 2, DT, S], F32R)
        wp_s = at("wp_s", 144, [P, 2, DT, V], F32R)
        res = at("res", 160, [P, B, DT, S])
        w_raw4 = at("w_raw4", 160, [P, 4, DT, V])
        probs = at("probs", 192, [P, DT, S])
        prep = [at(f"prep{i}", k, [P, 2, PC]) for i, k in enumerate((56, 60, 200))]
        bsum = [at(f"bsum{i}", 192 + 2 * i, [P, V]) for i in range(2)]
        w_hl = [at(f"w_hl{i}", 64 + 12 * i, [P, 2, W2], F32R) for i in range(NSLOT)]
        cms = at("cms", 112, [P, 2, DT, S], F32R)
        g_hl = [at(f"g_hl{i}", 128 + 4 * i, [P, 2, S], F32R) for i in range(NSLOT)]
        raw = [at(f"raw{i}", k, [P, W2]) for i, k in enumerate((200, 192, 144, 150))]
        gf = [at(f"gf{i}", 156 + 2 * i, [P, S]) for i in range(2)]
        yT = [at(f"yT{b}", 16 * b, [P, 2, DT, S], F32R) for b in range(B)]
        wd = [at(f"wd{i}", 64 + 8 * i, [P, 2, DT, KB], F32R) for i in range(2)]
        bup0 = at("bup0", 80, [P, B, V])
        yf = [at(f"yf{i}", 192 + 2 * i, [P, S]) for i in range(DT)]
        wu = [at(f"wu{i}", 88 + 8 * i, [P, 2, MT, V], F32R) for i in range(2)]
        z = [at("z0", 104, [P, DT, V]), at("z1", 136, [P, DT, V])]
        h_hl = [at(f"h_hl{i}", 112 + 8 * i, [P, 2, MT, S], F32R) for i in range(2)]
        bc = [at(f"bc{i}", 148 + 4 * i, [P, 2, V]) for i in range(2)]
        hf = [at(f"hf{i}", 156 + 2 * i, [P, S]) for i in range(2)]
        ident = at("ident", 206, [P, P])
        sm = at("sm", 206.5, [P, 224])
        NB_BIAS = 2 * HT + 3 * DT
        bias = sm[:, 0:NB_BIAS]
        bp, cb1 = bias[:, 0:DT], bias[:, DT:DT + HT]
        cb2 = bias[:, DT + HT:2 * DT + HT]
        mb1 = bias[:, 2 * DT + HT:2 * DT + 2 * HT]
        mb2 = bias[:, 2 * DT + 2 * HT:3 * DT + 2 * HT]
        cbias = sm[:, 44:60].rearrange("p (b d) -> p b d", b=B)
        codes_f = sm[:, 60:64]
        feat_f = sm[:, 64:68]
        rowmax = sm[:, 68:72]
        negmax = sm[:, 72:76]
        rowsum = sm[:, 76:80]
        rowinv = sm[:, 80:84]
        pp = sm[:, 84:124].rearrange("p (b n) -> p b n", b=B)
        stats = sm[:, 124:148].rearrange("p (t n) -> p t n", n=6)
        mv = sm[:, 148:164].rearrange("p (i t n) -> p i t n", i=2, n=2)
        rstd = sm[:, 164:172].rearrange("p (i t) -> p i t", i=2)
        nmr = sm[:, 172:180].rearrange("p (i t) -> p i t", i=2)
        mhalf = sm[:, 180:184]
        ve = sm[:, 184:192].rearrange("p (i t) -> p i t", i=2)
        codes_i = at("codes_i", 206.5 + 0.875, [P, B], I32)
        experts = at("experts", 206.5 + 0.875 + 1 / 32, [1, B], I32)
        feat_i = at("feat_i", 206.5 + 0.875 + 2 / 32, [P, DT], I32)

        wdu_split = nc.dram_tensor("wdu_split", (NPIECE, P, 2, PC), F32).ap()
        beta_bup = nc.dram_tensor("beta_bup", ((LAYERS - 1) * EXPERTS, V), F32).ap()

        psum = ctx.enter_context(nc.psum_tensor("psum", [P, BANKS, 512], F32))
        bank = [psum[:, i, :] for i in range(BANKS)]
        ACC = [bank[4 + d] for d in range(DT)]
        UP = bank[0:DT]
        DOWN = bank[4:4 + MT]
        TR = bank[6:8]

        def f(ap):
            return ap.bitcast(F32)

        s_w = [sem(f"weight_{n}_landed") for n in ("v", "p", "q", "k")]
        s_x = sem("x_rows_landed")
        s_small = sem("small_inputs_landed")
        s_idx = sem("experts_landed")
        s_ident = sem("identity_ready")
        s_iota = sem("iota_ready")
        s_cast = sem("codes_and_iota_cast")
        s_cbias = sem("cms_bias_ready")
        s_wp = sem("wp_hi_ready")
        s_wpl = sem("wp_split")
        bank_full = sem("bank_full")
        act_done = sem("act_done")
        dve_done = sem("dve_done")
        s_last_hi = sem("last_attention_hi_done")
        s_rmax = sem("row_max_found")
        s_nmax = sem("neg_row_max_ready")
        s_rinv = sem("row_sum_inverted")
        s_raw = [sem(f"raw_tile_landed_{i}") for i in range(NSLOT)]
        w_slot_free = sem("weight_slot_free")
        up_full = sem("up_bank_full")
        w_hi_done = sem("weight_hi_done")
        w_lo_done = sem("weight_lo_done")
        w_lo_pool = sem("weight_lo_done_pool")
        gelu_done = sem("gelu_done")
        g_hi_done = sem("g_hi_done")
        g_lo_done = sem("g_lo_done")
        s_acc1 = sem("cms_accumulated")
        s_acc2 = sem("modifier_accumulated")
        cms_hi_done = sem("cms_hi_done")
        cms_lo_done = sem("cms_lo_done")
        cms_added = sem("cms_added")
        mod_added = sem("modifier_added")
        y0_done = sem("y0_done")
        s_bsum_in = sem("betas_landed")
        s_bsum = sem("betas_summed")
        s_bsum_out = sem("beta_sums_stored")
        p_in = [sem(f"piece_landed_{i}") for i in range(PSLOT)]
        p_hi = sem("piece_hi_done")
        p_lo = sem("piece_lo_done")
        p_free = [sem(f"piece_slot_free_{i}") for i in range(PSLOT)]
        t_wd = [sem(f"down_weights_landed_{i}") for i in range(2)]
        t_wu = [sem(f"up_weights_landed_{i}") for i in range(2)]
        t_pp = [sem(f"unit_columns_landed_{i}") for i in range(B)]
        t_bc = [sem(f"unit_rows_landed_{i}") for i in range(2)]
        t_bup0 = sem("first_up_bias_landed")
        t_rows_full = sem("y0_rows_full")
        t_res_done = sem("y0_residual_done")
        t_y0hi = sem("y0_hi_done")
        t_y0lo = sem("y0_lo_done")
        t_yhi = sem("y_hi_done")
        t_ylo = sem("y_lo_done")
        t_yf = sem("y_scaled")
        t_down = sem("down_full")
        t_hf = sem("h_gelu_done")
        t_hhi = sem("h_hi_done")
        t_hlo = sem("h_lo_done")
        t_up = sem("up_full")
        t_z = sem("z_summed")
        t_bn = sem("z_stats_taken")
        t_mv = sem("mean_var_ready")
        t_ve = sem("var_eps_ready")
        t_rstd = sem("rstd_ready")
        t_nmr = sem("shift_ready")
        t_zn = sem("z_normalised")
        t_tr = sem("transposed_full")
        t_rmul = sem("row_scaled")
        t_res = sem("row_result_ready")
        t_vmul = sem("output_row_scaled_by_vector")
        t_vres = sem("output_row_ready_by_vector")
        s_half = sem("minus_half_ready")
        s_ident0 = sem("identity_cleared")
        s_out = sem("output_stored")

        J_WQ, J_WK, J_G, J_WV, J_X0, J_U0, J_VP, J_V0, J_S0 = (4 * i for i in range(9))
        J_LOOP = 36
        JX, JPT, JU, JPV, JV, JS = (J_LOOP + 4 * i for i in range(6))
        PER = 24
        J_PT3 = J_LOOP + 3 * PER
        J_PV3 = J_PT3 + DT
        J_END = J_PV3 + DT
        SLOTS0 = NSLOT
        PTILES = 3
        GF0 = 2
        Y0 = DT

        def w_ready(t, b, q=0):
            return (2 * HT - PTILES) * b + 4 * q + (t + 1 - PTILES)

        def pool_rows(u):
            return DT if u < 8 else 1 if u == 11 else 2

        def rows_before(u):
            return sum(pool_rows(v) for v in range(u))

        block = ctx.enter_context(nc.Block())

        @block.sync
        def _(sp):
            for i in (2, 3, 0):
                sp.dma_start(w_raw4[:, i, :, :], wts[i]).then_inc(s_w[i], 16)
            sp.dma_start(xrows[:, :, :], xin[0]).then_inc(s_x, 16)
            sp.dma_start(w_raw4[:, 1, :, :], wts[1]).then_inc(s_w[1], 16)
            sp.dma_start(bias, bias_in).then_inc(s_small, 16)
            sp.dma_start(codes_i[:, :], codes_in.to_broadcast([P, B])).then_inc(s_small, 16)
            NS = (LAYERS - 1) * EXPERTS
            sp.dma_start(bsum[0][0:NS, :], gb_all[0:NS, 1, :]).then_inc(s_bsum_in, 16)
            sp.dma_start(bsum[1][0:NS, :], bup_all[EXPERTS:EXPERTS + NS, :]).then_inc(s_bsum_in, 16)
            sp.dma_start(experts[:, :], experts_in).then_inc(s_idx, 16)
            sp.wait_ge(s_idx, 16)
            ex = [sp.value_load(experts[0:1, b:b + 1], min_val=0, max_val=EXPERTS - 1)
                  for b in range(B)]
            sp.wait_ge(s_bsum, 1)
            sp.dma_start(beta_bup, bsum[1][0:NS, :]).then_inc(s_bsum_out, 16)

            def pieces(phase):
                for c in range(PHASE + 2):
                    if c >= 2:
                        o = c - 2
                        i = o % PSLOT
                        sp.wait_ge(p_lo, phase * PHASE + (o + 1))
                        sp.dma_start(wdu_split[bass.ds(phase * PHASE + o, 1)].rearrange("o p e n -> (o p) e n"),
                                     prep[i][:, :, :]).then_inc(p_free[i], 16)
                    if c < PHASE:
                        i = c % PSLOT
                        sp.wait_ge(p_free[i], phase * (PHASE // PSLOT * 16) + 16 * (c // PSLOT + 1))
                        sp.dma_start(prep[i][:, 1, :], wdu_all[bass.ds(phase * PHASE + c, 1)]
                                     .rearrange("o p n -> (o p) n")).then_inc(p_in[i], 16)

            pieces(0)
            with sp.Fori(0, B - 1) as b:
                sp.wait_ge(bank_full, b * PER + (J_X0 + DT))
                sp.dma_start(xrows[:, :, :], xin[bass.ds(b + 1, 1)].rearrange("o p k n -> p (o k) n")).then_inc(s_x, 16)
                pieces(b + 1)
            sp.wait_ge(bank_full, J_PT3 + DT)
            for i in range(PSLOT):
                sp.wait_ge(p_free[i], 16 * (NPIECE // PSLOT + 1))
            with sp.Fori(0, B) as b:
                with sp.Fori(0, HT // NSLOT) as q:
                    for j in range(NSLOT):
                        if j == 2:
                            sp.wait_ge(bank_full, J_END)
                        sp.wait_ge(up_full, b * (2 * HT) + q * NSLOT + (j + 1))
                        sp.dma_start(raw[j][:, 0:W1], mlp1[bass.ds(q * NSLOT + j, 1)].rearrange("o p n -> (o p) n")).then_inc(s_raw[j], 16)
                with sp.Fori(0, HT // NSLOT) as q:
                    for j in range(NSLOT):
                        sp.wait_ge(up_full, b * (2 * HT) + q * NSLOT + (HT + j + 1))
                        sp.dma_start(raw[j][:, 0:W2], mlp2[bass.ds(q * NSLOT + j, 1)].rearrange("o p n -> (o p) n")).then_inc(s_raw[j], 16)

            split_sets = wdu_split.rearrange("(s c) p e n -> s c p e n", c=NPC)

            def unit_down(u):
                b = u % B
                if u >= 2:
                    sp.wait_ge(t_down, (u - 1) * MT)
                sp.dma_start(f(wd[u % 2][:, :, :, :].rearrange("p e (c k) n -> p e c (k n)", c=DT * KB // PC)),
                             split_sets[bass.ds(u // B * EXPERTS + ex[b], 1), 0:DT * KB // PC].rearrange("o c p e n -> p e (o c) n")).then_inc(t_wd[u % 2], 16)

            def unit_up(u):
                b = u % B
                if u >= 2:
                    sp.wait_ge(t_up, (u - 1) * DT)
                sp.dma_start(f(wu[u % 2][:, :, :, :]),
                             split_sets[bass.ds(u // B * EXPERTS + ex[b], 1), DT * KB // PC:NPC].rearrange("o c p e n -> p e (o c) n")).then_inc(t_wu[u % 2], 16)

            def unit_columns(u, layer, b):
                if u >= B:
                    sp.wait_ge(t_yf, (u - 4) * DT + DT)
                row = layer * EXPERTS + ex[b]
                sp.dma_start(pp[:, b, :], pp_all[bass.ds(row, 1)].rearrange("o p n -> (o p) n")).then_inc(t_pp[b], 16)

            def unit_rows(u, layer, b):
                if u >= 2:
                    sp.wait_ge(t_res, rows_before(u - 1))
                    if u - 2 >= 8:
                        sp.wait_ge(t_vres, (u - 9) * DT - (rows_before(u - 1) - rows_before(8)))
                row = layer * EXPERTS + ex[b]
                if layer == LAYERS - 1:
                    sp.dma_start(bc[b % 2][:, :, :], gb_all[bass.ds(row, 1)].to_broadcast([P, 2, V])).then_inc(t_bc[b % 2], 32)
                else:
                    sp.dma_start(bc[b % 2][:, 0, :], gb_all[bass.ds(row, 1), 0].to_broadcast([P, V])).then_inc(t_bc[b % 2], 16)
                    sp.dma_start(bc[b % 2][:, 1, :], beta_bup[bass.ds(row, 1)].to_broadcast([P, V])).then_inc(t_bc[b % 2], 16)

            TOT = 2 * HT * B
            for i in range(PSLOT):
                sp.wait_ge(p_free[i], 16 * (NPIECE // PSLOT + 1))
            sp.wait_ge(s_bsum_out, 16)
            sp.wait_ge(w_lo_done, (2 * HT - PTILES) * B)
            sp.wait_ge(w_slot_free, SLOTS0 + TOT - 2)
            unit_down(0)
            unit_down(1)
            for b in range(B):
                sp.dma_start(bup0[:, b, :], bup_all[bass.ds(ex[b], 1)].to_broadcast([P, V])).then_inc(t_bup0, 16)
                unit_columns(b, 0, b)
            unit_rows(0, 0, 0)
            unit_rows(1, 0, 1)
            sp.wait_ge(w_slot_free, SLOTS0 + TOT)
            unit_up(0)
            unit_up(1)
            for u in range(2, 14):
                if u < 12:
                    unit_down(u)
                    if u >= B:
                        unit_columns(u, u // B, u % B)
                if 4 <= u:
                    unit_rows(u - 2, (u - 2) // B, (u - 2) % B)
                if u < 12:
                    unit_up(u)
            for u in range(8, 12):
                for i in range(DT):
                    k = pool_rows(u)
                    if i < k:
                        sp.wait_ge(t_res, rows_before(u) + i + 1)
                    else:
                        sp.wait_ge(t_vres, (u - 8) * DT - (rows_before(u) - rows_before(8)) + i - k + 1)
                    sp.dma_start(out[u % B, :, i, :], res[:, u % B, i, :]).then_inc(s_out, 16)
            sp.wait_ge(s_out, 16 * B * DT)

        @block.tensor
        def _(pe):
            def mm3(ps, lw, rw, first, last):
                nc.tensor.matmul(ps, lw(0), rw(0), start=first, stop=False)
                nc.tensor.matmul(ps, lw(0), rw(1), start=False, stop=False)
                return nc.tensor.matmul(ps, lw(1), rw(0), start=False, stop=last)

            def bank_wait(n):
                pe.wait_ge(dve_done, n - (BANKS - 1))

            def transposes(n, const, src, wait=None):
                for d in range(DT):
                    if const + d >= BANKS:
                        bank_wait(n + d)
                    for i in range(DT):
                        if wait and d == 0:
                            wait(i)
                        ins = nc.tensor.transpose(bank[(const + d) % BANKS][:, i * P:(i + 1) * P],
                                                  src[:, i, d * P:(d + 1) * P], ident[:, :])
                    ins.then_inc(bank_full, 1)

            def product(n, const, lhs, rhs, ready_l, ready_r):
                for m in range(DT):
                    bank_wait(n + m)
                    for k in range(DT):
                        if m == 0:
                            if ready_l is not None:
                                pe.wait_ge(dve_done, ready_l + (k + 1))
                            if ready_r is not None:
                                pe.wait_ge(dve_done, ready_r + (k + 1))
                        ins = mm3(bank[(const + m) % BANKS],
                                  lambda e: lhs[:, e, k, m * P:(m + 1) * P], lambda e: rhs[:, e, k, :],
                                  k == 0, k == DT - 1)
                    ins.then_inc(bank_full, 1)

            pe.wait_ge(s_ident, 1)
            pe.wait_ge(s_w[2], 16)
            transposes(J_WQ, J_WQ, w_raw4[:, 2, :, :])
            pe.wait_ge(s_w[3], 16)
            transposes(J_WK, J_WK, w_raw4[:, 3, :, :])
            product(J_G, J_G, wqT, wkT, J_WQ, J_WK)
            pe.wait_ge(s_w[0], 16)
            transposes(J_WV, J_WV, w_raw4[:, 0, :, :])
            pe.wait_ge(s_x, 16)
            transposes(J_X0, J_X0, xrows[:, :, :])
            product(J_U0, J_U0, g_w, xT, J_G, J_X0)
            pe.wait_ge(s_wpl, 1)
            product(J_VP, J_VP, wvT, wp_s, J_WV, None)
            product(J_V0, J_V0, xT, vp_w, None, J_VP)
            product(J_S0, J_S0, uT, xT, J_U0, None)
            with pe.Fori(0, B - 1) as b:
                n = b * PER
                pe.wait_ge(s_x, b * 16 + 32)
                transposes(n + JX, JX, xrows[:, :, :])
                for i in range(DT):
                    pe.wait_ge(dve_done, n + (JX - DT + i + 1))
                    for d in range(DT):
                        if i == 0:
                            bank_wait(n + JPT + d)
                        ins = nc.tensor.transpose(bank[(JPT + d) % BANKS][:, i * P:(i + 1) * P],
                                                  probs[:, i, d * P:(d + 1) * P], ident[:, :])
                        if i == DT - 1:
                            ins.then_inc(bank_full, 1)
                product(n + JU, JU, g_w, xT, None, n + JX)
                product(n + JPV, JPV, v_n, pT, None, n + JPT)
                product(n + JV, JV, xT, vp_w, None, None)
                product(n + JS, JS, uT, xT, n + JU, None)
            pe.wait_ge(dve_done, J_PT3)
            for d in range(DT):
                bank_wait(J_PT3 + d)
                for i in range(DT):
                    ins = nc.tensor.transpose(bank[(J_PT3 + d) % BANKS][:, i * P:(i + 1) * P],
                                              probs[:, i, d * P:(d + 1) * P], ident[:, :])
                    if d == DT - 1 and i == 0:
                        ins.then_inc(w_slot_free, SLOTS0)
                    if d == DT - 1 and i == 1:
                        ins.then_inc(up_full, SLOTS0)
                    if d == DT - 1 and i == 2:
                        ins.then_inc(y0_done, Y0)
                    if d == DT - 2 and i == 0:
                        ins.then_inc(g_lo_done, GF0)
                ins.then_inc(bank_full, 1)
            product(J_PV3, J_PV3, v_n, pT, None, J_PT3)
            pe.wait_ge(dve_done, J_END)

            with pe.Fori(0, B) as b:
                def up_a(t, width, first, last):
                    s = t % NSLOT
                    for k in range(DT):
                        ins = mm3(bank[s], lambda e: w_hl[s][:, e, k * P:(k + 1) * P],
                                  lambda e: a_all[:, bass.ds(b, 1), e, k, :].rearrange("p o n -> p (o n)"),
                                  first and k == 0, last and k == DT - 1)
                    return ins

                def up_c(t, wait=False):
                    s = t % NSLOT
                    for k in range(DT):
                        if wait:
                            pe.wait_ge(cms_lo_done, b * DT + (k + 1))
                        ins = mm3(bank[s], lambda e: w_hl[s][:, e, (DT + k) * P:(DT + k + 1) * P],
                                  lambda e: cms[:, e, k, :], False, k == DT - 1)
                    return ins

                def down(t, q, off, first=False, last=False, done=None):
                    s = t % NSLOT
                    pe.wait_ge(g_lo_done, b * (2 * HT) + q * NSLOT + (GF0 + t + 1))
                    for d in range(DT):
                        ins = mm3(ACC[d], lambda e: w_hl[s][:, e, off + d * P:off + (d + 1) * P],
                                  lambda e: g_hl[s][:, e, :], first, last)
                        if done is not None and d < DT - 1:
                            ins.then_inc(done, 1)
                        elif done is not None:
                            ins.then_inc(done, 1)
                    return ins

                def down_free(t, q, off, **kw):
                    down(t, q, off, **kw).then_inc(w_slot_free, 1)

                D1, D2 = DT * P, 2 * DT * P
                pe.wait_ge(w_lo_pool, b * PTILES + 1)
                up_a(0, W1, True, True).then_inc(up_full, 1)
                pe.wait_ge(w_lo_pool, b * PTILES + 2)
                up_a(1, W1, True, True).then_inc(up_full, 1)
                pe.wait_ge(w_lo_pool, b * PTILES + 3)
                up_a(2, W1, True, True).then_inc(up_full, 1)
                pe.wait_ge(y0_done, b * DT + Y0)
                down_free(0, 0, D1, first=True)
                pe.wait_ge(w_lo_done, w_ready(3, b))
                up_a(3, W1, True, True).then_inc(up_full, 1)
                down_free(1, 0, D1)
                with pe.Fori(0, HT // NSLOT - 1) as q:
                    for j in range(NSLOT):
                        pe.wait_ge(w_lo_done, w_ready(4 + j, b, q))
                        up_a(4 + j, W1, True, True).then_inc(up_full, 1)
                        down_free(2 + j, q, D1)
                pe.wait_ge(w_lo_done, w_ready(16, b))
                up_a(16, W2, True, False)
                down_free(14, 0, D1)
                pe.wait_ge(w_lo_done, w_ready(17, b))
                up_a(17, W2, True, False)
                down(15, 0, D1, last=True).then_inc(w_slot_free, 1)
                pe.wait_ge(w_lo_done, w_ready(18, b))
                up_a(18, W2, True, False)
                up_c(16, wait=True).then_inc(up_full, 1)
                up_c(17).then_inc(up_full, 1)
                up_c(18).then_inc(up_full, 1)
                pe.wait_ge(cms_added, (b + 1) * DT)
                down_free(16, 0, D2, first=True)
                pe.wait_ge(w_lo_done, w_ready(19, b))
                up_a(19, W2, True, False)
                up_c(19).then_inc(up_full, 1)
                down_free(17, 0, D2)
                with pe.Fori(0, HT // NSLOT - 1) as q:
                    for j in range(NSLOT):
                        pe.wait_ge(w_lo_done, w_ready(20 + j, b, q))
                        up_a(20 + j, W2, True, False)
                        up_c(20 + j).then_inc(up_full, 1)
                        down_free(18 + j, q, D2)
                down_free(30, 0, D2)
                down_free(31, 0, D2, last=True)

            def y0_to_rows(b):
                if b == B - 1:
                    pe.wait_ge(y0_done, Y0 + B * DT)
                for i in range(DT):
                    if b:
                        pe.wait_ge(t_res_done, (b - 1) * DT + i + 1)
                    for d in range(DT):
                        ins = nc.tensor.transpose(UP[i][:, d * P:(d + 1) * P],
                                                  res[:, b, d, i * P:(i + 1) * P], ident[:, :])
                    ins.then_inc(t_rows_full, 1)

            def t_down_mm(u, b):
                pe.wait_ge(t_wd[u % 2], 16 * (u // 2 + 1))
                for m in range(MT):
                    if u > 0:
                        pe.wait_ge(t_hf, (u - 1) * MT + m + 1)
                    else:
                        pe.wait_ge(mod_added, (B - 1) * DT + m + 1)
                    for k in range(DT):
                        if m == 0 and u < B:
                            pe.wait_ge(t_y0lo, u * DT + (k + 1))
                        elif m == 0:
                            pe.wait_ge(t_ylo, (u - B) * DT + (k + 1))
                        ins = mm3(DOWN[m], lambda e: wd[b % 2][:, e, k, m * P:(m + 1) * P],
                                  lambda e: yT[b][:, e, k, :], k == 0, k == DT - 1)
                    ins.then_inc(t_down, 1)

            def t_up_mm(u, b):
                pe.wait_ge(t_wu[u % 2], 16 * (u // 2 + 1))
                for i in range(DT):
                    if isinstance(u, int) and u == 0:
                        pe.wait_ge(t_res_done, B * DT)
                    else:
                        pe.wait_ge(t_z, u * DT - DT + i + 1)
                    for k in range(MT):
                        if i == 0:
                            pe.wait_ge(t_hlo, u * MT + (k + 1))
                        ins = mm3(UP[i], lambda e: h_hl[b % 2][:, e, k, i * P:(i + 1) * P],
                                  lambda e: wu[b % 2][:, e, k, :], k == 0, k == MT - 1)
                    ins.then_inc(t_up, 1)

            def t_transpose(u, b):
                for d in range(DT):
                    if u * DT + d >= 2:
                        pe.wait_ge(t_yf, u * DT + (d - 1))
                    for i in range(DT):
                        if d == 0:
                            pe.wait_ge(t_zn, u * DT + (i + 1))
                        ins = nc.tensor.transpose(TR[d % 2][:, i * P:(i + 1) * P],
                                                  z[b % 2][:, i, d * P:(d + 1) * P], ident[:, :])
                    ins.then_inc(t_tr, 1)

            y0_to_rows(0)
            for s in range(13):
                if s < 12:
                    t_down_mm(s, s % B)
                if s == 0:
                    y0_to_rows(1)
                if s == 1:
                    y0_to_rows(2)
                    y0_to_rows(3)
                if 1 <= s:
                    t_up_mm(s - 1, (s - 1) % B)
                if 2 <= s < 10:
                    t_transpose(s - 2, (s - 2) % B)

        @block.scalar
        def _(act):
            def hi_jobs(n, const, dst, keep=None, scale=None, after=None):
                for m in range(DT):
                    act.wait_ge(bank_full, n + (m + 1))
                    src = bank[(const + m) % BANKS]
                    if keep is not None:
                        nc.scalar.copy(keep(m), src)
                    if scale is None:
                        nc.scalar.copy(dst(m), src).then_inc(act_done, 1)
                    else:
                        nc.scalar.activation(dst(m), src, ACT.Identity, scale=scale).then_inc(act_done, 1)
                    if after is not None:
                        after(m)

            def piece_hi(phase, c):
                i = c % PSLOT
                act.wait_ge(p_in[i], phase * (PHASE // PSLOT * 16) + 16 * (c // PSLOT + 1))
                nc.scalar.copy(prep[i][:, 0, :].bitcast(F32R), prep[i][:, 1, :]).then_inc(p_hi, 1)

            def exp_jobs(n, const):
                for m in range(DT):
                    act.wait_ge(s_nmax, n_s(n, m))
                    nc.scalar.activation(probs[:, m, :], bank[(const + m) % BANKS], ACT.Exp,
                                         bias=negmax[:, m:m + 1], accum_out=rowsum[:, m:m + 1]).then_inc(act_done, 1)

            def n_s(seq, m):
                return seq * DT + (m + 1)

            hi_jobs(J_WQ, J_WQ, lambda m: wqT[:, 0, m, :])
            hi_jobs(J_WK, J_WK, lambda m: wkT[:, 0, m, :])
            hi_jobs(J_G, J_G, lambda m: g_w[:, 0, m, :])
            hi_jobs(J_WV, J_WV, lambda m: wvT[:, 0, m, :])
            hi_jobs(J_X0, J_X0, lambda m: xT[:, 0, m, :], keep=lambda m: res[:, 0, m, :])
            act.wait_ge(s_w[1], 16)
            nc.scalar.copy(wp_s[:, 0, :, :], w_raw4[:, 1, :, :]).then_inc(s_wp, 1)
            hi_jobs(J_U0, J_U0, lambda m: uT[:, 0, m, :], scale=SCALE, after=lambda m: piece_hi(0, m))
            hi_jobs(J_VP, J_VP, lambda m: vp_w[:, 0, m, :], after=lambda m: piece_hi(0, DT + m))
            piece_hi(0, 2 * DT)
            hi_jobs(J_V0, J_V0, lambda m: v_n[:, 0, m, :])
            act.wait_ge(s_bsum_out, 16)
            exp_jobs(0, J_S0)

            act.wait_ge(s_small, 32)

            def attn_jobs(n, const, b, after):
                for m in range(DT):
                    act.wait_ge(bank_full, n + (m + 1))
                    dst = a_all[:, bass.ds(b, 1), 0, m, :].rearrange("p o n -> p (o n)")
                    nc.scalar.activation(dst, bank[(const + m) % BANKS], ACT.Identity,
                                         bias=bp[:, m:m + 1]).then_inc(act_done, 1)
                    after(m)

            with act.Fori(0, B - 1) as b:
                n = b * PER

                hi_jobs(n + JX, JX, lambda m: xT[:, 0, m, :],
                        keep=lambda m: res[:, bass.ds(b + 1, 1), m, :].rearrange("p o n -> p (o n)"))
                hi_jobs(n + JPT, JPT, lambda m: pT[:, 0, m, :])
                hi_jobs(n + JU, JU, lambda m: uT[:, 0, m, :], scale=SCALE, after=lambda m: piece_hi(b + 1, m))
                attn_jobs(n + JPV, JPV, b, lambda m: piece_hi(b + 1, DT + m))
                piece_hi(b + 1, 2 * DT)
                hi_jobs(n + JV, JV, lambda m: v_n[:, 0, m, :])
                exp_jobs(b + 1, JS)
            hi_jobs(J_PT3, J_PT3, lambda m: pT[:, 0, m, :])

            with act.Fori(0, B) as b:
                def gelu(t, q, bias_ap):
                    s = t % NSLOT
                    act.wait_ge(up_full, b * (2 * HT) + q * NSLOT + (SLOTS0 + t + 1))
                    act.wait_ge(g_lo_done, b * (2 * HT) + q * NSLOT + (GF0 + t - 1))
                    nc.scalar.activation(gf[t % 2][:, :], bank[s], ACT.Gelu, bias=bias_ap).then_inc(gelu_done, 1)
                    act.wait_ge(gelu_done, b * (2 * HT) + q * NSLOT + (t + 1))
                    nc.scalar.copy(g_hl[s][:, 0, :], gf[t % 2][:, :]).then_inc(g_hi_done, 1)

                def w_hi(t, q, width, n):
                    s = t % NSLOT
                    act.wait_ge(s_raw[s], (b * (2 * HT // NSLOT) + q + (n + 1)) * 16)
                    act.wait_ge(w_slot_free, b * (2 * HT) + q * NSLOT + (t + 1))
                    nc.scalar.copy(w_hl[s][:, 0, 0:width], raw[s][:, 0:width]).then_inc(w_hi_done, 1)

                for t in range(PTILES):
                    w_hi(t, 0, W1, 0)
                with act.Fori(0, HT // NSLOT - 1) as q:
                    for j in range(NSLOT):
                        gelu(j, q, cb1[:, bass.ds(q * NSLOT + j, 1)])
                        w_hi(j + 3, q, W1, (j + 3) // NSLOT)
                for t in range(12, 16):
                    gelu(t, 0, cb1[:, t:t + 1])
                    w_hi(t + 3, 0, W1 if t + 3 < HT else W2, (t + 3) // NSLOT)
                for d in range(DT):
                    act.wait_ge(w_slot_free, b * (2 * HT) + (SLOTS0 + HT))
                    nc.scalar.activation(cms[:, 0, d, :], ACC[d], ACT.Identity,
                                         bias=cbias[:, bass.ds(b, 1), d]).then_inc(cms_hi_done, 1)
                with act.Fori(0, HT // NSLOT - 1) as q:
                    for j in range(NSLOT):
                        gelu(HT + j, q, mb1[:, bass.ds(q * NSLOT + j, 1)])
                        w_hi(HT + j + 3, q, W2, (HT + j + 3) // NSLOT)
                for t in range(28, 32):
                    gelu(t, 0, mb1[:, t - HT:t - HT + 1])
                    if t + 3 < 32:
                        w_hi(t + 3, 0, W2, (t + 3) // NSLOT)

            TOT = 2 * HT * B

            def y0_hi(b):
                act.wait_ge(y0_done, Y0 + (b + 1) * DT)
                for d in range(DT):
                    nc.scalar.copy(yT[b][:, 0, d, :], res[:, b, d, :]).then_inc(t_y0hi, 1)

            def z_norm(u):
                for i in range(DT):
                    act.wait_ge(t_nmr, u + 1)
                    nc.scalar.activation(z[u % 2][:, i, :], z[u % 2][:, i, :], ACT.Identity,
                                         scale=rstd[:, u % 2, i:i + 1], bias=nmr[:, u % 2, i:i + 1]).then_inc(t_zn, 1)

            def h_gelu(u):
                for m in range(MT):
                    act.wait_ge(t_down, u * MT + m + 1)
                    if m == 0:
                        act.wait_ge(t_pp[u % B], 16 * (u // B + 1))
                    if u > 0:
                        act.wait_ge(t_hlo, (u - 1) * MT + m + 1)
                    nc.scalar.activation(hf[m][:, :], DOWN[m], ACT.Gelu, bias=pp[:, u % B, 8 + m:9 + m]).then_inc(t_hf, 1)
                for m in range(MT):
                    act.wait_ge(t_hf, u * MT + m + 1)
                    if u >= 2:
                        act.wait_ge(t_up, (u - 1) * DT)
                    nc.scalar.copy(h_hl[u % 2][:, 0, m, :], hf[m][:, :]).then_inc(t_hhi, 1)

            def y_scale(u):
                for d in range(DT):
                    act.wait_ge(t_tr, u * DT + d + 1)
                    if u:
                        act.wait_ge(t_ylo, (u - 1) * DT + d + 1)
                    nc.scalar.activation(yf[d][:, :], TR[d % 2], ACT.Identity,
                                         scale=pp[:, u % B, d:d + 1], bias=pp[:, u % B, 4 + d:5 + d]).then_inc(t_yf, 1)
                for d in range(DT):
                    act.wait_ge(t_yf, u * DT + d + 1)
                    nc.scalar.copy(yT[u % B][:, 0, d, :], yf[d][:, :]).then_inc(t_yhi, 1)

            act.wait_ge(up_full, SLOTS0 + TOT)
            for b in range(B - 1):
                y0_hi(b)
            for s in range(14):
                if 2 <= s:
                    z_norm(s - 2)
                if s < 12:
                    h_gelu(s)
                if s == 0:
                    y0_hi(B - 1)
                if 2 <= s < 10:
                    y_scale(s - 2)

        @block.vector
        def _(dve):
            def lo_jobs(n, const, tile, scale=None):
                for m in range(DT):
                    dve.wait_ge(act_done, n + (m + 1))
                    src = bank[(const + m) % BANKS]
                    if scale is None:
                        nc.vector.tensor_tensor(tile[:, 1, m, :], src, f(tile[:, 0, m, :]), ALU.subtract).then_inc(dve_done, 1)
                    else:
                        nc.vector.scalar_tensor_tensor(out=tile[:, 1, m, :], in0=src, scalar=scale, in1=f(tile[:, 0, m, :]),
                                                       op0=ALU.mult, op1=ALU.subtract).then_inc(dve_done, 1)

            def softmax_jobs(n, const, seq):
                for m in range(DT):
                    dve.wait_ge(bank_full, n + (m + 1))
                    nc.vector.reduce_max(rowmax[:, m:m + 1], bank[(const + m) % BANKS], AX.X).then_inc(s_rmax, 1)
                    dve.wait_ge(s_rmax, seq * DT + (m + 1))
                    nc.vector.tensor_scalar(negmax[:, m:m + 1], rowmax[:, m:m + 1], -1.0, None, ALU.mult).then_inc(s_nmax, 1)
                for m in range(DT):
                    dve.wait_ge(act_done, n + (m + 1))
                    nc.vector.reciprocal(rowinv[:, m:m + 1], rowsum[:, m:m + 1]).then_inc(s_rinv, 1)
                    dve.wait_ge(s_rinv, seq * DT + (m + 1))
                    nc.vector.tensor_scalar(probs[:, m, :], probs[:, m, :], rowinv[:, m:m + 1], None, ALU.mult).then_inc(dve_done, 1)

            def attn_lo(n, const, b):
                for m in range(DT):
                    dve.wait_ge(act_done, n + (m + 1))
                    hi, lo = (a_all[:, bass.ds(b, 1), e, m, :].rearrange("p o n -> p (o n)") for e in range(2))
                    nc.vector.scalar_tensor_tensor(out=lo, in0=bank[(const + m) % BANKS], scalar=bp[:, m:m + 1], in1=f(hi),
                                                   op0=ALU.add, op1=ALU.subtract).then_inc(dve_done, 1)

            lo_jobs(J_WQ, J_WQ, wqT)
            lo_jobs(J_WK, J_WK, wkT)
            lo_jobs(J_G, J_G, g_w)
            dve.wait_ge(s_bsum_in, 32)
            NS = (LAYERS - 1) * EXPERTS
            nc.vector.tensor_tensor(bsum[1][0:NS, :], bsum[1][0:NS, :], bsum[0][0:NS, :], ALU.add).then_inc(s_bsum, 1)
            lo_jobs(J_WV, J_WV, wvT)
            lo_jobs(J_X0, J_X0, xT)
            dve.wait_ge(s_wp, 1)
            nc.vector.tensor_tensor(wp_s[:, 1, :, :], w_raw4[:, 1, :, :], f(wp_s[:, 0, :, :]), ALU.subtract).then_inc(s_wpl, 1)
            lo_jobs(J_U0, J_U0, uT, scale=SCALE)
            dve.wait_ge(s_small, 32)
            dve.wait_ge(s_iota, 1)
            nc.vector.tensor_copy(codes_f, codes_i[:, :]).then_inc(s_cast, 1)
            nc.vector.tensor_copy(feat_f, feat_i[:, :]).then_inc(s_cast, 1)
            dve.wait_ge(s_cast, 2)
            for b in range(B):
                nc.vector.scalar_tensor_tensor(out=cbias[:, b, :], in0=feat_f, scalar=codes_f[:, b:b + 1], in1=cb2,
                                               op0=ALU.is_equal, op1=ALU.add).then_inc(s_cbias, 1)
            lo_jobs(J_VP, J_VP, vp_w)
            lo_jobs(J_V0, J_V0, v_n)
            softmax_jobs(J_S0, J_S0, 0)
            with dve.Fori(0, B - 1) as b:
                n = b * PER
                lo_jobs(n + JX, JX, xT)
                lo_jobs(n + JPT, JPT, pT)
                lo_jobs(n + JU, JU, uT, scale=SCALE)
                attn_lo(n + JPV, JPV, b)
                lo_jobs(n + JV, JV, v_n)
                softmax_jobs(n + JS, JS, b + 1)
            lo_jobs(J_PT3, J_PT3, pT)
            for i in range(2):
                dve.wait_ge(p_free[i], 16 * (NPIECE // PSLOT + 1))
            for m in range(DT):
                dve.wait_ge(bank_full, J_PV3 + m + 1)
                src = bank[(J_PV3 + m) % BANKS]
                nc.vector.tensor_scalar(a_all[:, B - 1, 0, m, :], src, bp[:, m:m + 1], None, ALU.add).then_inc(s_last_hi, 1)
                dve.wait_ge(s_last_hi, m + 1)
                nc.vector.scalar_tensor_tensor(out=a_all[:, B - 1, 1, m, :], in0=src, scalar=bp[:, m:m + 1], in1=f(a_all[:, B - 1, 0, m, :]),
                                               op0=ALU.add, op1=ALU.subtract).then_inc(dve_done, 1)

            with dve.Fori(0, B) as b:
                def seq_res(d):
                    return res[:, bass.ds(b, 1), d, :].rearrange("p o n -> p (o n)")

                def g_lo(t, q):
                    s = t % NSLOT
                    dve.wait_ge(g_hi_done, b * (2 * HT) + q * NSLOT + (t + 1))
                    nc.vector.tensor_tensor(g_hl[s][:, 1, :], gf[t % 2][:, :], f(g_hl[s][:, 0, :]), ALU.subtract).then_inc(g_lo_done, 1)

                def w_lo(t, q, width):
                    s = t % NSLOT
                    dve.wait_ge(w_hi_done, b * (2 * HT) + q * NSLOT + (t + 1))
                    nc.vector.tensor_tensor(w_hl[s][:, 1, 0:width], raw[s][:, 0:width], f(w_hl[s][:, 0, 0:width]), ALU.subtract).then_inc(w_lo_done, 1)

                with dve.Fori(0, HT // NSLOT - 1) as q:
                    for j in range(NSLOT):
                        g_lo(j, q)
                        w_lo(j + 3, q, W1)
                for t in range(12, 16):
                    g_lo(t, 0)
                    w_lo(t + 3, 0, W1 if t + 3 < HT else W2)
                for d in range(DT):
                    dve.wait_ge(cms_hi_done, b * DT + (d + 1))
                    nc.vector.scalar_tensor_tensor(out=cms[:, 1, d, :], in0=ACC[d], scalar=cbias[:, bass.ds(b, 1), d],
                                                   in1=f(cms[:, 0, d, :]), op0=ALU.add, op1=ALU.subtract).then_inc(cms_lo_done, 1)
                for d in range(DT):
                    nc.vector.scalar_tensor_tensor(out=seq_res(d), in0=ACC[d], scalar=cbias[:, bass.ds(b, 1), d],
                                                   in1=seq_res(d), op0=ALU.add, op1=ALU.add).then_inc(cms_added, 1)
                with dve.Fori(0, HT // NSLOT - 1) as q:
                    for j in range(NSLOT):
                        g_lo(HT + j, q)
                        w_lo(HT + j + 3, q, W2)
                for t in range(28, 32):
                    g_lo(t, 0)
                    if t + 3 < 32:
                        w_lo(t + 3, 0, W2)
                for d in range(DT):
                    dve.wait_ge(w_slot_free, b * (2 * HT) + (SLOTS0 + 2 * HT))
                    nc.vector.scalar_tensor_tensor(out=seq_res(d), in0=ACC[d], scalar=mb2[:, d:d + 1],
                                                   in1=seq_res(d), op0=ALU.add, op1=ALU.add).then_inc(mod_added, 1)
                for d in range(DT):
                    dve.wait_ge(mod_added, b * DT + (d + 1))
                    nc.vector.tensor_scalar(seq_res(d), seq_res(d), 0.0, 1.0, ALU.max, ALU.min).then_inc(y0_done, 1)

            def y0_rows(b):
                dve.wait_ge(t_bup0, 16 * B)
                dve.wait_ge(t_y0lo, (b + 1) * DT)
                dve.wait_ge(t_rows_full, (b + 1) * DT)
                for i in range(DT):
                    nc.vector.tensor_tensor(res[:, b, i, :], UP[i], bup0[:, b, :], ALU.add).then_inc(t_res_done, 1)

            def shift(u):
                dve.wait_ge(t_rstd, u + 1)
                nc.vector.scalar_tensor_tensor(out=nmr[:, u % 2, :], in0=mv[:, u % 2, :, 0], scalar=-1.0, in1=rstd[:, u % 2, :],
                                               op0=ALU.mult, op1=ALU.mult).then_inc(t_nmr, 1)

            def h_lo(u):
                for m in range(MT):
                    dve.wait_ge(t_hhi, u * MT + m + 1)
                    nc.vector.tensor_tensor(h_hl[u % 2][:, 1, m, :], hf[m][:, :], f(h_hl[u % 2][:, 0, m, :]), ALU.subtract).then_inc(t_hlo, 1)

            def z_stats(u):
                for i in range(DT + 2):
                    if i < DT:
                        dve.wait_ge(t_up, u * DT + i + 1)
                        if u >= B:
                            dve.wait_ge(t_res, (u - B) * DT + i + 1)
                        if u >= 2:
                            if i < pool_rows(u - 2):
                                dve.wait_ge(t_rmul, rows_before(u - 2) + i + 1)
                            dve.wait_ge(t_tr, min((u - 1) * DT, 8 * DT))
                        nc.vector.tensor_tensor(z[u % 2][:, i, :], UP[i], res[:, u % B, i, :], ALU.add).then_inc(t_z, 1)
                    if 1 <= i < DT + 1:
                        k = i - 1
                        dve.wait_ge(t_z, u * DT + k + 1)
                        if u >= 1:
                            dve.wait_ge(t_mv, (u - 1) * DT + k + 1)
                        nc.vector.bn_stats(stats[:, k, :], z[u % 2][:, k, :]).then_inc(t_bn, 1)
                    if i >= 2:
                        k = i - 2
                        dve.wait_ge(t_bn, u * DT + k + 1)
                        if k == 0 and u >= 2:
                            dve.wait_ge(t_nmr, u - 1)
                            dve.wait_ge(t_ve, u - 1)
                        nc.vector.bn_aggr(mv[:, u % 2, k, :], stats[:, k, :]).then_inc(t_mv, 1)

            def y_lo(u):
                for d in range(DT):
                    dve.wait_ge(t_yhi, u * DT + d + 1)
                    nc.vector.tensor_tensor(yT[u % B][:, 1, d, :], yf[d][:, :], f(yT[u % B][:, 0, d, :]), ALU.subtract).then_inc(t_ylo, 1)

            def out_rows(u):
                dve.wait_ge(t_bc[u % 2], 32 * (u // 2 + 1))
                mine = range(pool_rows(u), DT)
                for i in mine:
                    dve.wait_ge(t_zn, u * DT + i + 1)
                    nc.vector.tensor_tensor(res[:, u % B, i, :], z[u % 2][:, i, :], bc[u % 2][:, 0, :], ALU.mult).then_inc(t_vmul, 1)
                for i in mine:
                    n = (u - 8) * DT - (rows_before(u) - rows_before(8)) + i - pool_rows(u) + 1
                    dve.wait_ge(t_vmul, n)
                    nc.vector.tensor_tensor(res[:, u % B, i, :], res[:, u % B, i, :], bc[u % 2][:, 1, :], ALU.add).then_inc(t_vres, 1)

            for s in range(14):
                if 2 <= s:
                    shift(s - 2)
                if s == 0:
                    y0_rows(0)
                if s < 12:
                    h_lo(s)
                if s == 0:
                    y0_rows(1)
                if s == 1:
                    y0_rows(2)
                    y0_rows(3)
                if 1 <= s < 13:
                    z_stats(s - 1)
                if 2 <= s < 10:
                    y_lo(s - 2)
                if 10 <= s:
                    out_rows(s - 2)

        @block.gpsimd
        def _(pool):
            nc.gpsimd.memset(ident[:, :], 0.0).then_inc(s_ident0, 1)
            pool.wait_ge(s_ident0, 1)
            nc.gpsimd.affine_select(out=ident[:, :], in_=ident[:, :], compare_op=ALU.not_equal, fill=1.0, base=0,
                                    pattern=[[-1, P]], channel_multiplier=1).then_inc(s_ident, 1)
            nc.gpsimd.iota(feat_i[:, :], pattern=[[P, DT]], base=0, channel_multiplier=1).then_inc(s_iota, 1)
            nc.gpsimd.memset(mhalf, -0.5).then_inc(s_half, 1)

            for i in range(PSLOT):
                nc.gpsimd.memset(sm[:, 192 + i:193 + i], 0.0).then_inc(p_free[i], 16)
            with pool.Fori(0, B) as phase:
                for c in range(PHASE):
                    i = c % PSLOT
                    pool.wait_ge(p_hi, phase * PHASE + (c + 1))
                    nc.gpsimd.tensor_tensor(prep[i][:, 1, :], prep[i][:, 1, :], prep[i][:, 0, :], ALU.subtract).then_inc(p_lo, 1)

            with pool.Fori(0, B) as b:
                for t in range(PTILES):
                    pool.wait_ge(w_hi_done, b * (2 * HT) + (t + 1))
                    nc.gpsimd.tensor_tensor(w_hl[t][:, 1, 0:W1], raw[t][:, 0:W1], f(w_hl[t][:, 0, 0:W1]), ALU.subtract).then_inc(w_lo_pool, 1)

            for b in range(B):
                for d in range(DT):
                    pool.wait_ge(t_y0hi, b * DT + d + 1)
                    nc.gpsimd.tensor_tensor(yT[b][:, 1, d, :], res[:, b, d, :], f(yT[b][:, 0, d, :]), ALU.subtract).then_inc(t_y0lo, 1)

            pool.wait_ge(s_half, 1)
            for u in range(12):
                i2 = u % 2
                pool.wait_ge(t_mv, (u + 1) * DT)
                if u >= 2:
                    pool.wait_ge(t_zn, (u - 1) * DT)
                nc.gpsimd.tensor_scalar(ve[:, i2, :], mv[:, i2, :, 1], EPS, 1.0, ALU.add, ALU.mult).then_inc(t_ve, 1)
                pool.wait_ge(t_ve, u + 1)
                nc.gpsimd.tensor_tensor(rstd[:, i2, :], ve[:, i2, :], mhalf, ALU.pow).then_inc(t_rstd, 1)
                pool.wait_ge(t_bc[i2], 32 * (u // 2 + 1))
                for i in range(pool_rows(u)):
                    pool.wait_ge(t_zn, u * DT + i + 1)
                    nc.gpsimd.tensor_tensor(res[:, u % B, i, :], z[i2][:, i, :], bc[i2][:, 0, :], ALU.mult).then_inc(t_rmul, 1)
                    pool.wait_ge(t_rmul, rows_before(u) + i + 1)
                    nc.gpsimd.tensor_tensor(res[:, u % B, i, :], res[:, u % B, i, :], bc[i2][:, 1, :], ALU.add).then_inc(t_res, 1)


_OUT = "out_dram"


def kernel(**inputs):
    import numpy as np
    import concourse.bacc as bacc
    from concourse.bass_utils import run_bass_kernel_spmd

    a = {k: np.asarray(v) for k, v in inputs.items()}

    def rows(w):
        return np.ascontiguousarray(w.reshape(-1, P, w.shape[-1]).transpose(1, 0, 2))

    def cols(v):
        return v.reshape(-1, P).T

    def up_tiles(w):
        k, t = w.shape[0] // P, w.shape[1] // P
        return w.reshape(k, P, t, P).transpose(2, 1, 0, 3).reshape(t, P, k * P)

    wts = np.stack([rows(a["L0_cond_" + n]) for n in ("Wv", "Wp", "Wq", "Wk")])
    mlp1 = np.concatenate([up_tiles(a["L0_cond_cW1"]), a["L0_cond_cW2"].reshape(HT, P, V)], axis=2)
    mlp2 = np.concatenate([up_tiles(a["L0_cond_mW1"]), a["L0_cond_mW2"].reshape(HT, P, V)], axis=2)
    bias = np.concatenate([cols(a["L0_cond_" + n]) for n in ("bp", "cb1", "cb2", "mb1", "mb2")], axis=1)
    names = [("L1", "ln_w", "ln_b"), ("L2", "gamma", "beta"), ("L3", "gamma", "beta")]
    wdu, pp, gb, bup = [], [], [], []
    for l, g, bt in names:
        for e in range(EXPERTS):
            w = np.concatenate([rows(a[f"{l}_cond_W_{n}"][e]).reshape(P, -1) for n in ("down", "up")], axis=1)
            wdu.append(w.reshape(P, NPC, PC).transpose(1, 0, 2))
            pp.append(np.concatenate([cols(a[f"{l}_cond_{g}"][e]), cols(a[f"{l}_cond_{bt}"][e]),
                                      cols(a[f"{l}_cond_b_down"][e])], axis=1))
            gb.append(np.stack([a[f"{l}_cond_{g}"][e], a[f"{l}_cond_{bt}"][e]]))
            bup.append(a[f"{l}_cond_b_up"][e])
    arrays = {
        "wts": wts, "x": np.stack([rows(a["x"][b]) for b in range(B)]), "bias": bias,
        "codes": a["itok_B_17_1546"].reshape(1, B), "experts": a["itok_B_1_2"].reshape(1, B),
        "mlp1": mlp1, "mlp2": mlp2, "wdu": np.concatenate(wdu), "pp": np.stack(pp),
        "gb": np.stack(gb), "bup": np.stack(bup),
    }
    arrays = {k + "_dram": np.ascontiguousarray(v) for k, v in arrays.items()}
    nc = bacc.Bacc("TRN2", target_bir_lowering=False, num_devices=1)
    args = [nc.dram_tensor(k, v.shape, mybir.dt.from_np(v.dtype), kind="ExternalInput").ap()
            for k, v in arrays.items()]
    args.append(nc.dram_tensor(_OUT, (B, P, DT, V), F32, kind="ExternalOutput").ap())
    build(nc, *args)
    r = run_bass_kernel_spmd(nc, [arrays], core_ids=[0])
    got = r.results[0][_OUT]
    return np.ascontiguousarray(got.transpose(0, 2, 1, 3)).reshape(B, S, V)
```

```python
from contextlib import ExitStack

import concourse.bass as bass
from concourse import mybir

F32 = mybir.dt.float32
F32R = mybir.dt.float32r
I32 = mybir.dt.int32
ALU = mybir.AluOpType
ACT = mybir.ActivationFunctionType
AX = mybir.AxisListType

P = 128
B = 4
S = 512
V = 512
H = 4 * V
KB = 256
LAYERS = 3
EXPERTS = 3
DT = V // P
MT = KB // P
HT = H // P
SCALE = V ** -0.5
EPS = 1e-5
W1 = DT * P + V
W2 = 2 * DT * P + V
NSLOT = 4
PC = 512
NPC = (DT * KB + MT * V) // PC
NPIECE = LAYERS * EXPERTS * NPC
PHASE = NPIECE // B
PSLOT = 3
XPOS = 1
BANKS = 8
KiB = 1024


def build(nc, wts, xin, bias_in, codes_in, experts_in, mlp1, mlp2, wdu_all, pp_all, gb_all,
          bup_all, out):
    ctx = ExitStack()
    with ctx:
        base = -(-nc.sbuf_base // 64) * 64

        def at(name, kib, shape, dt=F32):
            return nc.alloc_sbuf_tensor_at(name, shape, dt, offset=base + int(kib * KiB))

        def sem(name):
            return ctx.enter_context(nc.semaphore(name))

        a_all = at("a_all", 0, [P, B, 2, DT, S], F32R)
        wqT = at("wqT", 0, [P, 2, DT, V], F32R)
        wkT = at("wkT", 16, [P, 2, DT, V], F32R)
        wvT = at("wvT", 32, [P, 2, DT, V], F32R)
        g_w = at("g_w", 64, [P, 2, DT, V], F32R)
        vp_w = at("vp_w", 80, [P, 2, DT, V], F32R)
        xT = at("xT", 96, [P, 2, DT, S], F32R)
        uT = at("uT", 112, [P, 2, DT, S], F32R)
        v_n = at("v_n", 128, [P, 2, DT, V], F32R)
        pT = at("pT", 144, [P, 2, DT, S], F32R)
        wp_s = at("wp_s", 144, [P, 2, DT, V], F32R)
        wq_raw, wk_raw, wv_raw, wp_raw = (at(f"w{n}_raw", 112 + 8 * i, [P, DT, V]) for i, n in enumerate("qkvp"))
        res = at("res", 160, [P, B, DT, S])
        probs = at("probs", 192, [P, DT, S])
        prep = [at(f"prep{i}", k, [P, 2, PC]) for i, k in enumerate((56, 60, 200))]
        bsum = [at(f"bsum{i}", 192 + 2 * i, [P, V]) for i in range(2)]
        w_hl = [at(f"w_hl{i}", 64 + 12 * i, [P, 2, W2], F32R) for i in range(NSLOT)]
        cms = at("cms", 144, [P, 2, DT, S], F32R)
        g_hl = [at(f"g_hl{i}", 128 + 4 * i, [P, 2, S], F32R) for i in range(NSLOT)]
        raw = [at(f"raw{i}", k, [P, W2]) for i, k in enumerate((200, 192, 112, 118))]
        gf = [at(f"gf{i}", 124 + 2 * i, [P, S]) for i in range(2)]
        yT = [at(f"yT{b}", 16 * b, [P, 2, DT, S], F32R) for b in range(B)]
        wd = [at(f"wd{i}", 64 + 8 * i, [P, 2, DT, KB], F32R) for i in range(2)]
        bup0 = at("bup0", 80, [P, B, V])
        yf = [at(f"yf{i}", 192 + 2 * i, [P, S]) for i in range(DT)]
        wu = [at(f"wu{i}", 88 + 8 * i, [P, 2, MT, V], F32R) for i in range(2)]
        z = [at("z0", 104, [P, DT, V]), at("z1", 136, [P, DT, V])]
        h_hl = [at(f"h_hl{i}", 112 + 8 * i, [P, 2, MT, S], F32R) for i in range(2)]
        bc = [at(f"bc{i}", 148 + 4 * i, [P, 2, V]) for i in range(2)]
        hf = [at(f"hf{i}", 156 + 2 * i, [P, S]) for i in range(2)]
        ident = at("ident", 206, [P, P])
        sm = at("sm", 206.5, [P, 224])
        NB_BIAS = 2 * HT + 3 * DT
        bias = sm[:, 0:NB_BIAS]
        bp, cb1 = bias[:, 0:DT], bias[:, DT:DT + HT]
        cb2 = bias[:, DT + HT:2 * DT + HT]
        mb1 = bias[:, 2 * DT + HT:2 * DT + 2 * HT]
        mb2 = bias[:, 2 * DT + 2 * HT:3 * DT + 2 * HT]
        cbias = sm[:, 44:60].rearrange("p (b d) -> p b d", b=B)
        codes_f = sm[:, 60:64]
        feat_f = sm[:, 64:68]
        rowmax = sm[:, 68:72]
        negmax = sm[:, 72:76]
        rowsum = sm[:, 76:80]
        rowinv = sm[:, 80:84]
        pp = sm[:, 84:124].rearrange("p (b n) -> p b n", b=B)
        stats = sm[:, 124:148].rearrange("p (t n) -> p t n", n=6)
        mv = sm[:, 148:164].rearrange("p (i t n) -> p i t n", i=2, n=2)
        rstd = sm[:, 164:172].rearrange("p (i t) -> p i t", i=2)
        nmr = sm[:, 172:180].rearrange("p (i t) -> p i t", i=2)
        mhalf = sm[:, 180:184]
        ve = sm[:, 184:192].rearrange("p (i t) -> p i t", i=2)
        codes_i = at("codes_i", 206.5 + 0.875, [P, B], I32)
        experts = at("experts", 206.5 + 0.875 + 1 / 32, [1, B], I32)
        feat_i = at("feat_i", 206.5 + 0.875 + 2 / 32, [P, DT], I32)

        wdu_split = nc.dram_tensor("wdu_split", (NPIECE, P, 2, PC), F32).ap()
        beta_bup = nc.dram_tensor("beta_bup", ((LAYERS - 1) * EXPERTS, V), F32).ap()

        psum = ctx.enter_context(nc.psum_tensor("psum", [P, BANKS, 512], F32))
        bank = [psum[:, i, :] for i in range(BANKS)]
        ACC = [bank[4 + d] for d in range(DT)]
        UP = bank[0:DT]

        def down_bank(u, m):
            return bank[4 + 2 * (u % 2) + m]

        def tr_bank(u, d):
            if u == 11:
                return UP[d]
            return bank[4 + 2 * ((u % 2) ^ (1 if d < 2 else 0)) + d % 2]

        def f(ap):
            return ap.bitcast(F32)

        s_w = [sem(f"weight_{n}_landed") for n in ("v", "p")]
        s_whi = [sem(f"weight_{n}_hi_done") for n in ("v", "p")]
        s_wsplit = [sem(f"weight_{n}_split") for n in ("v", "p")]
        qk_hi = sem("weights_qk_rows_hi_done")
        qk_split = sem("weights_qk_rows_split")
        x_hi = sem("x_transposed_hi_done")
        x_split = sem("x_transposed_split")
        s_wqk = [[sem(f"weight_{n}_rows_landed_{i}") for i in range(DT)] for n in ("q", "k")]
        s_x = sem("x_transposed_landed")
        s_small = sem("small_inputs_landed")
        s_idx = sem("experts_landed")
        s_ident = sem("identity_ready")
        s_iota = sem("iota_ready")
        s_cast = sem("codes_and_iota_cast")
        s_cbias = sem("cms_bias_ready")
        bank_full = sem("bank_full")
        act_done = sem("act_done")
        dve_done = sem("dve_done")
        s_last_hi = sem("last_attention_hi_done")
        s_rmax = sem("row_max_found")
        s_nmax = sem("neg_row_max_ready")
        s_rinv = sem("row_sum_inverted")
        s_raw = [sem(f"raw_tile_landed_{i}") for i in range(NSLOT)]
        w_slot_free = sem("weight_slot_free")
        up_full = sem("up_bank_full")
        w_hi_done = sem("weight_hi_done")
        w_lo_done = sem("weight_lo_done")
        w_lo_pool = sem("weight_lo_done_pool")
        gelu_done = sem("gelu_done")
        g_hi_done = sem("g_hi_done")
        g_lo_done = sem("g_lo_done")
        s_acc1 = sem("cms_accumulated")
        s_acc2 = sem("modifier_accumulated")
        cms_hi_done = sem("cms_hi_done")
        cms_lo_done = sem("cms_lo_done")
        cms_added = sem("cms_added")
        mod_added = sem("modifier_added")
        y0_done = sem("y0_done")
        s_bsum_in = sem("betas_landed")
        s_bsum = sem("betas_summed")
        s_bsum_out = sem("beta_sums_stored")
        p_in = [sem(f"piece_landed_{i}") for i in range(PSLOT)]
        p_hi = sem("piece_hi_done")
        p_lo = sem("piece_lo_done")
        p_free = [sem(f"piece_slot_free_{i}") for i in range(PSLOT)]
        t_wd = [sem(f"down_weights_landed_{i}") for i in range(2)]
        t_wu = [sem(f"up_weights_landed_{i}") for i in range(2)]
        t_pp = [sem(f"unit_columns_landed_{i}") for i in range(B)]
        t_bc = [sem(f"unit_rows_landed_{i}") for i in range(2)]
        t_bup0 = sem("first_up_bias_landed")
        t_rows_full = sem("y0_rows_full")
        t_res_done = sem("y0_residual_done")
        t_y0hi = sem("y0_hi_done")
        t_y0lo = sem("y0_lo_done")
        t_yhi = sem("y_hi_done")
        t_ylo = sem("y_lo_done")
        t_yf = sem("y_scaled")
        t_down = sem("down_full")
        t_hf = sem("h_gelu_done")
        t_hhi = sem("h_hi_done")
        t_hlo = sem("h_lo_done")
        t_up = sem("up_full")
        t_z = sem("z_summed")
        t_bn = sem("z_stats_taken")
        s_half = sem("minus_half_ready")
        t_ve = sem("var_eps_ready")
        t_mv = sem("mean_var_ready")
        t_rstd = sem("rstd_ready")
        t_nmr = sem("shift_ready")
        t_zn = sem("z_normalised")
        t_tr = sem("transposed_full")
        t_rmul = sem("row_scaled")
        t_res = sem("row_result_ready")
        t_yv = sem("y_scaled_by_vector")
        t_znv = sem("z_normalised_by_vector")
        s_ident0 = sem("identity_cleared")
        s_out = sem("output_stored")

        LOW, HIGH = 0, DT
        J_G, J_U0, J_VP, J_S0 = (DT * i for i in range(4))
        J_LOOP = 4 * DT
        JV, JPV, JU, JS = (J_LOOP + DT * i for i in (0, 2, 3, 4))
        JPT = JV + DT - 1
        PER = 5 * DT
        J_V3 = J_LOOP + (B - 1) * PER
        J_PT3 = J_V3 + DT - 1
        J_PV3 = J_V3 + 2 * DT
        SLOTS0 = NSLOT
        PTILES = 3
        GF0 = 2
        Y0 = DT

        def w_ready(t, b, q=0):
            return (2 * HT - PTILES) * b + 4 * q + (t + 1 - PTILES)

        def nmr_count(u, i):
            return u + 1 if u < FINE else FINE + (u - FINE) * 2 + i // 2 + 1

        def y_ready(u, d):
            if u < 11:
                return t_yf, u * DT + d + 1
            by_act, by_dve = LAST_BY
            return (t_yf, u * DT + by_act.index(d) + 1) if d in by_act else (t_yv, by_dve.index(d) + 1)

        FINE = 10
        LAST_BY = (0, 2), (1, 3)

        block = ctx.enter_context(nc.Block())

        @block.sync
        def _(sp):
            for k in range(DT):
                for i, w in enumerate((wq_raw, wk_raw)):
                    sp.dma_start(w[:, k, :], wts[2 + i, :, k, :]).then_inc(s_wqk[i][k], 16)
            sp.dma_start(res[:, 0, :, :], xin[0]).then_inc(s_x, 16)
            for i, w in enumerate((wv_raw, wp_raw)):
                sp.dma_start(w[:, :, :], wts[i]).then_inc(s_w[i], 16)
            sp.dma_start(bias, bias_in).then_inc(s_small, 16)
            sp.dma_start(codes_i[:, :], codes_in.to_broadcast([P, B])).then_inc(s_small, 16)
            NS = (LAYERS - 1) * EXPERTS
            sp.dma_start(bsum[0][0:NS, :], gb_all[0:NS, 1, :]).then_inc(s_bsum_in, 16)
            sp.dma_start(bsum[1][0:NS, :], bup_all[EXPERTS:EXPERTS + NS, :]).then_inc(s_bsum_in, 16)
            sp.dma_start(experts[:, :], experts_in).then_inc(s_idx, 16)
            sp.wait_ge(s_idx, 16)
            ex = [sp.value_load(experts[0:1, b:b + 1], min_val=0, max_val=EXPERTS - 1)
                  for b in range(B)]

            def bsum_store():
                sp.wait_ge(s_bsum, 1)
                sp.dma_start(beta_bup, bsum[1][0:NS, :]).then_inc(s_bsum_out, 16)

            def pieces(phase, other):
                for c in range(PHASE + 2):
                    if c >= 2:
                        o = c - 2
                        i = o % PSLOT
                        sp.wait_ge(p_lo, phase * PHASE + (o + 1))
                        sp.dma_start(wdu_split[bass.ds(phase * PHASE + o, 1)].rearrange("o p e n -> (o p) e n"),
                                     prep[i][:, :, :]).then_inc(p_free[i], 16)
                    if c < PHASE:
                        i = c % PSLOT
                        sp.wait_ge(p_free[i], phase * (PHASE // PSLOT * 16) + 16 * (c // PSLOT + 1))
                        sp.dma_start(prep[i][:, 1, :], wdu_all[bass.ds(phase * PHASE + c, 1)]
                                     .rearrange("o p n -> (o p) n")).then_inc(p_in[i], 16)
                    if c == XPOS:
                        other()

            pieces(0, bsum_store)
            with sp.Fori(0, B - 1) as b:
                def x_next():
                    sp.wait_ge(x_split, (b + 1) * DT)
                    sp.dma_start(res[:, bass.ds(b + 1, 1), :, :].rearrange("p o k n -> p (o k) n"),
                                 xin[bass.ds(b + 1, 1)].rearrange("o p k n -> p (o k) n")).then_inc(s_x, 16)

                pieces(b + 1, x_next)
            sp.wait_ge(bank_full, J_PT3 + DT)
            for i in range(PSLOT):
                sp.wait_ge(p_free[i], 16 * (NPIECE // PSLOT + 1))
            with sp.Fori(0, B) as b:
                with sp.Fori(0, HT // NSLOT) as q:
                    for j in range(NSLOT):
                        sp.wait_ge(up_full, b * (2 * HT) + q * NSLOT + (j + 1))
                        sp.dma_start(raw[j][:, 0:W1], mlp1[bass.ds(q * NSLOT + j, 1)].rearrange("o p n -> (o p) n")).then_inc(s_raw[j], 16)
                with sp.Fori(0, HT // NSLOT) as q:
                    for j in range(NSLOT):
                        sp.wait_ge(up_full, b * (2 * HT) + q * NSLOT + (HT + j + 1))
                        sp.dma_start(raw[j][:, 0:W2], mlp2[bass.ds(q * NSLOT + j, 1)].rearrange("o p n -> (o p) n")).then_inc(s_raw[j], 16)

            split_sets = wdu_split.rearrange("(s c) p e n -> s c p e n", c=NPC)

            def unit_down(u):
                b = u % B
                if u >= 2:
                    sp.wait_ge(t_down, (u - 1) * MT)
                sp.dma_start(f(wd[u % 2][:, :, :, :].rearrange("p e (c k) n -> p e c (k n)", c=DT * KB // PC)),
                             split_sets[bass.ds(u // B * EXPERTS + ex[b], 1), 0:DT * KB // PC].rearrange("o c p e n -> p e (o c) n")).then_inc(t_wd[u % 2], 16)

            def unit_up(u):
                b = u % B
                if u >= 2:
                    sp.wait_ge(t_up, (u - 1) * DT)
                sp.dma_start(f(wu[u % 2][:, :, :, :]),
                             split_sets[bass.ds(u // B * EXPERTS + ex[b], 1), DT * KB // PC:NPC].rearrange("o c p e n -> p e (o c) n")).then_inc(t_wu[u % 2], 16)

            def unit_columns(u, layer, b):
                if u >= B:
                    sp.wait_ge(t_yf, (u - 4) * DT + DT)
                row = layer * EXPERTS + ex[b]
                sp.dma_start(pp[:, b, :], pp_all[bass.ds(row, 1)].rearrange("o p n -> (o p) n")).then_inc(t_pp[b], 16)

            def unit_rows(u, layer, b):
                if u >= 2:
                    sp.wait_ge(t_res, (u - 1) * DT)
                row = layer * EXPERTS + ex[b]
                sp.dma_start(bc[b % 2][:, 0, :], gb_all[bass.ds(row, 1), 0].to_broadcast([P, V])).then_inc(t_bc[b % 2], 16)
                sp.dma_start(bc[b % 2][:, 1, :], beta_bup[bass.ds(row, 1)].to_broadcast([P, V])).then_inc(t_bc[b % 2], 16)

            TOT = 2 * HT * B
            for i in range(PSLOT):
                sp.wait_ge(p_free[i], 16 * (NPIECE // PSLOT + 1))
            sp.wait_ge(s_bsum_out, 16)
            sp.wait_ge(w_lo_done, (2 * HT - PTILES) * B)
            sp.wait_ge(w_slot_free, SLOTS0 + TOT - 2)
            unit_down(0)
            unit_down(1)
            for b in range(B):
                sp.dma_start(bup0[:, b, :], bup_all[bass.ds(ex[b], 1)].to_broadcast([P, V])).then_inc(t_bup0, 16)
                unit_columns(b, 0, b)
            unit_rows(0, 0, 0)
            unit_rows(1, 0, 1)
            sp.wait_ge(w_slot_free, SLOTS0 + TOT)
            unit_up(0)
            unit_up(1)
            for u in range(2, 14):
                if u < 12:
                    unit_down(u)
                    if u >= B:
                        unit_columns(u, u // B, u % B)
                if 4 <= u < 10:
                    unit_rows(u - 2, (u - 2) // B, (u - 2) % B)
                if u < 12:
                    unit_up(u)
            for u in (8, 9):
                sp.wait_ge(t_yf, (u + 1) * DT)
                sp.dma_start(out[u % B], res[:, u % B, :, :]).then_inc(s_out, 16)
            for u in (10, 11):
                for d in range(DT):
                    sp.wait_ge(*y_ready(u, d))
                    sp.dma_start(out[u % B, :, d, :], res[:, u % B, d, :]).then_inc(s_out, 16)
            sp.wait_ge(s_out, 16 * (2 + 2 * DT))

        @block.tensor
        def _(pe):
            def mm3(ps, lw, rw, first, last, signals=()):
                for i, (el, er) in enumerate(((0, 0), (0, 1), (1, 0))):
                    ins = nc.tensor.matmul(ps, lw(el), rw(er), start=first and i == 0, stop=last and i == 2)
                    if signals:
                        ins.then_inc(*signals[i])
                return ins

            def product(n, group, lhs, rhs, ready=None, free=None, tiles=range(DT), signals=()):
                for m in tiles:
                    if free is not None:
                        free(m)
                    elif ready is None or m > 0:
                        pe.wait_ge(dve_done, n + m - (BANKS - 1))
                    for k in range(DT):
                        if m == 0 and ready is not None:
                            ready(k)
                        ins = mm3(bank[group + m],
                                  lambda e: lhs[:, e, k, m * P:(m + 1) * P], lambda e: rhs[:, e, k, :],
                                  k == 0, k == DT - 1, signals if m == 0 and k == 0 else ())
                    ins.then_inc(bank_full, 1)

            def split(sem_, before, per_k=1):
                return lambda k: pe.wait_ge(sem_, before + per_k * (k + 1))

            def known(m):
                pass

            def v_jobs(n, tiles, ready=None):
                job = n if tiles[0] < DT - 1 else n + DT
                product(job, LOW, xT, vp_w, ready=ready, free=lambda m: pe.wait_ge(act_done, n - DT + (m + 1)), tiles=tiles)

            def pT_jobs(n):
                for d in range(DT):
                    for i in range(DT):
                        ins = nc.tensor.transpose(bank[HIGH + d][:, i * P:(i + 1) * P],
                                                  probs[:, i, d * P:(d + 1) * P], ident[:, :])
                    ins.then_inc(bank_full, 1)

            def pv_ready(n):
                return lambda k: pe.wait_ge(dve_done, n + (k + 1) + (1 if k == DT - 1 else 0))

            product(J_G, HIGH, wqT, wkT, ready=split(qk_split, 0, per_k=2), free=known)
            pe.wait_ge(x_split, DT)
            product(J_U0, LOW, g_w, xT, ready=split(dve_done, J_G), free=known)
            pe.wait_ge(s_wsplit[0], 1)
            pe.wait_ge(s_wsplit[1], 1)
            product(J_VP, HIGH, wvT, wp_s)
            product(J_S0, LOW, uT, xT, ready=split(dve_done, J_U0))
            pe.wait_ge(s_ident, 1)
            with pe.Fori(0, B - 1) as b:
                n = b * PER
                v_jobs(n + JV, (0, 1, 2), ready=split(dve_done, J_VP))
                pe.wait_ge(dve_done, n + J_LOOP)
                pT_jobs(n + JPT)
                v_jobs(n + JV, (3,))
                product(n + JPV, LOW, v_n, pT, ready=pv_ready(n + JPT))
                product(n + JU, HIGH, g_w, xT, ready=split(x_split, (b + 1) * DT))
                product(n + JS, LOW, uT, xT, ready=split(dve_done, n + JU))
            v_jobs(J_V3, (0, 1, 2))
            pe.wait_ge(dve_done, J_V3)
            pT_jobs(J_PT3)
            v_jobs(J_V3, (3,))
            product(J_PV3, HIGH, v_n, pT, ready=pv_ready(J_PT3), free=known,
                    signals=((w_slot_free, SLOTS0), (up_full, SLOTS0), (g_lo_done, GF0)))

            with pe.Fori(0, B) as b:
                def up_a(t, width, first, last):
                    s = t % NSLOT
                    for k in range(DT):
                        ins = mm3(bank[s], lambda e: w_hl[s][:, e, k * P:(k + 1) * P],
                                  lambda e: a_all[:, bass.ds(b, 1), e, k, :].rearrange("p o n -> p (o n)"),
                                  first and k == 0, last and k == DT - 1)
                    return ins

                def up_c(t, wait=False):
                    s = t % NSLOT
                    for k in range(DT):
                        if wait:
                            pe.wait_ge(cms_lo_done, b * DT + (k + 1))
                        ins = mm3(bank[s], lambda e: w_hl[s][:, e, (DT + k) * P:(DT + k + 1) * P],
                                  lambda e: cms[:, e, k, :], False, k == DT - 1)
                    return ins

                def down(t, q, off, first=False, last=False, done=None):
                    s = t % NSLOT
                    pe.wait_ge(g_lo_done, b * (2 * HT) + q * NSLOT + (GF0 + t + 1))
                    for d in range(DT):
                        ins = mm3(ACC[d], lambda e: w_hl[s][:, e, off + d * P:off + (d + 1) * P],
                                  lambda e: g_hl[s][:, e, :], first, last)
                        if done is not None and d < DT - 1:
                            ins.then_inc(done, 1)
                        elif done is not None:
                            ins.then_inc(done, 1)
                    return ins

                def down_free(t, q, off, **kw):
                    down(t, q, off, **kw).then_inc(w_slot_free, 1)

                D1, D2 = DT * P, 2 * DT * P
                pe.wait_ge(w_lo_pool, b * PTILES + 1)
                up_a(0, W1, True, True).then_inc(up_full, 1)
                pe.wait_ge(w_lo_pool, b * PTILES + 2)
                up_a(1, W1, True, True).then_inc(up_full, 1)
                pe.wait_ge(w_lo_pool, b * PTILES + 3)
                up_a(2, W1, True, True).then_inc(up_full, 1)
                pe.wait_ge(y0_done, b * DT + Y0)
                down_free(0, 0, D1, first=True)
                pe.wait_ge(w_lo_done, w_ready(3, b))
                up_a(3, W1, True, True).then_inc(up_full, 1)
                down_free(1, 0, D1)
                with pe.Fori(0, HT // NSLOT - 1) as q:
                    for j in range(NSLOT):
                        pe.wait_ge(w_lo_done, w_ready(4 + j, b, q))
                        up_a(4 + j, W1, True, True).then_inc(up_full, 1)
                        down_free(2 + j, q, D1)
                pe.wait_ge(w_lo_done, w_ready(16, b))
                up_a(16, W2, True, False)
                down_free(14, 0, D1)
                pe.wait_ge(w_lo_done, w_ready(17, b))
                up_a(17, W2, True, False)
                down(15, 0, D1, last=True).then_inc(w_slot_free, 1)
                pe.wait_ge(w_lo_done, w_ready(18, b))
                up_a(18, W2, True, False)
                up_c(16, wait=True).then_inc(up_full, 1)
                up_c(17).then_inc(up_full, 1)
                up_c(18).then_inc(up_full, 1)
                pe.wait_ge(cms_added, (b + 1) * DT)
                down_free(16, 0, D2, first=True)
                pe.wait_ge(w_lo_done, w_ready(19, b))
                up_a(19, W2, True, False)
                up_c(19).then_inc(up_full, 1)
                down_free(17, 0, D2)
                with pe.Fori(0, HT // NSLOT - 1) as q:
                    for j in range(NSLOT):
                        pe.wait_ge(w_lo_done, w_ready(20 + j, b, q))
                        up_a(20 + j, W2, True, False)
                        up_c(20 + j).then_inc(up_full, 1)
                        down_free(18 + j, q, D2)
                down_free(30, 0, D2)
                down_free(31, 0, D2, last=True)

            def y0_to_rows(b):
                if b == B - 1:
                    pe.wait_ge(y0_done, Y0 + B * DT)
                for i in range(DT):
                    if b == 1:
                        pe.wait_ge(t_res_done, i + 1)
                    if b > 1:
                        pe.wait_ge(t_z, (b - 2) * DT + i + 1)
                    for d in range(DT):
                        ins = nc.tensor.transpose(UP[i][:, d * P:(d + 1) * P],
                                                  res[:, b, d, i * P:(i + 1) * P], ident[:, :])
                    ins.then_inc(t_rows_full, 1)

            def t_down_mm(u, b):
                pe.wait_ge(t_wd[u % 2], 16 * (u // 2 + 1))
                for m in range(MT):
                    if u < 2:
                        pe.wait_ge(mod_added, (B - 1) * DT + u * MT + m + 1)
                    elif u == 2:
                        pe.wait_ge(t_hf, (u - 2) * MT + m + 1)
                    else:
                        pe.wait_ge(t_yf, (u - 3) * DT + m + 1)
                    for k in range(DT):
                        if m == 0 and u < B:
                            pe.wait_ge(t_y0lo, u * DT + (k + 1))
                        elif m == 0:
                            pe.wait_ge(t_ylo, (u - B) * DT + (k + 1))
                        ins = mm3(down_bank(u, m), lambda e: wd[b % 2][:, e, k, m * P:(m + 1) * P],
                                  lambda e: yT[b][:, e, k, :], k == 0, k == DT - 1)
                    ins.then_inc(t_down, 1)

            def t_up_mm(u, b):
                pe.wait_ge(t_wu[u % 2], 16 * (u // 2 + 1))
                for i in range(DT):
                    if u < 3:
                        pe.wait_ge(t_res_done, (u + 1) * DT + i + 1)
                    else:
                        pe.wait_ge(t_z, (u - 1) * DT + i + 1)
                    for k in range(MT):
                        if i == 0:
                            pe.wait_ge(t_hlo, u * MT + (k + 1))
                        ins = mm3(UP[i], lambda e: h_hl[b % 2][:, e, k, i * P:(i + 1) * P],
                                  lambda e: wu[b % 2][:, e, k, :], k == 0, k == MT - 1)
                    ins.then_inc(t_up, 1)

            def t_transpose(u, b):
                for d in range(DT):
                    if u == 11:
                        pe.wait_ge(t_z, 12 * DT)
                    elif u == 10 and d >= 2:
                        pe.wait_ge(t_yf, (u - 1) * DT + d - 1)
                    elif d >= 2:
                        pe.wait_ge(t_hf, (u + 2) * MT + d - 1)
                    elif u:
                        pe.wait_ge(t_yf, (u - 1) * DT + d + 3)
                    else:
                        pe.wait_ge(t_hf, MT + d + 1)
                    for i in range(DT):
                        if d == 0 and u == 11:
                            if i % 2:
                                pe.wait_ge(t_znv, i // 2 + 1)
                            else:
                                pe.wait_ge(t_zn, 11 * DT + i // 2 + 1)
                        elif d == 0:
                            pe.wait_ge(t_zn, u * DT + (i + 1))
                        ins = nc.tensor.transpose(tr_bank(u, d)[:, i * P:(i + 1) * P],
                                                  z[b % 2][:, i, d * P:(d + 1) * P], ident[:, :])
                    ins.then_inc(t_tr, 1)

            y0_to_rows(0)
            for s in range(14):
                if s < 12:
                    t_down_mm(s, s % B)
                if s == 0:
                    y0_to_rows(1)
                if 1 <= s < 13:
                    t_up_mm(s - 1, (s - 1) % B)
                if 1 <= s < 3:
                    y0_to_rows(s + 1)
                if 2 <= s:
                    t_transpose(s - 2, (s - 2) % B)

        @block.scalar
        def _(act):
            def hi_jobs(n, group, dst, scale=None, after=None, tiles=range(DT)):
                for m in tiles:
                    act.wait_ge(bank_full, n + (m + 1))
                    if scale is None:
                        nc.scalar.copy(dst(m), bank[group + m]).then_inc(act_done, 1)
                    else:
                        nc.scalar.activation(dst(m), bank[group + m], ACT.Identity, scale=scale).then_inc(act_done, 1)
                    if after is not None:
                        after(m)

            def x_hi_parts(seq):
                act.wait_ge(s_x, seq * 16 + 16)
                for k in range(DT):
                    nc.scalar.copy(xT[:, 0, k, :], res[:, bass.ds(seq, 1), k, :].rearrange("p o n -> p (o n)")).then_inc(x_hi, 1)

            def piece_hi(phase, c):
                i = c % PSLOT
                act.wait_ge(p_in[i], phase * (PHASE // PSLOT * 16) + 16 * (c // PSLOT + 1))
                nc.scalar.copy(prep[i][:, 0, :].bitcast(F32R), prep[i][:, 1, :]).then_inc(p_hi, 1)

            def exp_jobs(n, group):
                for m in range(DT):
                    act.wait_ge(s_nmax, n_s(n, m))
                    nc.scalar.activation(probs[:, m, :], bank[group + m], ACT.Exp,
                                         bias=negmax[:, m:m + 1], accum_out=rowsum[:, m:m + 1]).then_inc(act_done, 1)

            def n_s(seq, m):
                return seq * DT + (m + 1)

            for k in range(DT):
                for i, (w, raw_w) in enumerate(((wqT, wq_raw), (wkT, wk_raw))):
                    act.wait_ge(s_wqk[i][k], 16)
                    nc.scalar.copy(w[:, 0, k, :], raw_w[:, k, :]).then_inc(qk_hi, 1)
            x_hi_parts(0)
            hi_jobs(J_G, HIGH, lambda m: g_w[:, 0, m, :])
            for i, (w, raw_w) in enumerate(((wvT, wv_raw), (wp_s, wp_raw))):
                act.wait_ge(s_w[i], 16)
                nc.scalar.copy(w[:, 0, :, :], raw_w[:, :, :]).then_inc(s_whi[i], 1)
            hi_jobs(J_U0, LOW, lambda m: uT[:, 0, m, :], scale=SCALE, after=lambda m: piece_hi(0, m))
            hi_jobs(J_VP, HIGH, lambda m: vp_w[:, 0, m, :], after=lambda m: piece_hi(0, DT + m))
            piece_hi(0, 2 * DT)
            act.wait_ge(s_bsum_out, 16)
            exp_jobs(0, LOW)

            act.wait_ge(s_small, 32)

            def attn_jobs(n, b, after):
                for m in range(DT):
                    act.wait_ge(bank_full, n + (m + 1))
                    dst = a_all[:, bass.ds(b, 1), 0, m, :].rearrange("p o n -> p (o n)")
                    nc.scalar.activation(dst, bank[LOW + m], ACT.Identity,
                                         bias=bp[:, m:m + 1]).then_inc(act_done, 1)
                    after(m)

            with act.Fori(0, B - 1) as b:
                n = b * PER

                def piece(c, m):
                    if m < PSLOT:
                        piece_hi(b + 1, c + m)

                hi_jobs(n + JV, LOW, lambda m: v_n[:, 0, m, :], after=lambda m: piece(0, m), tiles=(0, 1, 2))
                hi_jobs(n + JPT, HIGH, lambda m: pT[:, 0, m, :])
                hi_jobs(n + JV + DT, LOW, lambda m: v_n[:, 0, m, :], tiles=(3,))
                x_hi_parts(b + 1)
                attn_jobs(n + JPV, b, lambda m: piece(PSLOT, m))
                hi_jobs(n + JU, HIGH, lambda m: uT[:, 0, m, :], scale=SCALE, after=lambda m: piece(2 * PSLOT, m))
                exp_jobs(b + 1, LOW)
            hi_jobs(J_V3, LOW, lambda m: v_n[:, 0, m, :], tiles=(0, 1, 2))
            hi_jobs(J_PT3, HIGH, lambda m: pT[:, 0, m, :])
            hi_jobs(J_V3 + DT, LOW, lambda m: v_n[:, 0, m, :], tiles=(3,))

            with act.Fori(0, B) as b:
                def gelu(t, q, bias_ap):
                    s = t % NSLOT
                    act.wait_ge(up_full, b * (2 * HT) + q * NSLOT + (SLOTS0 + t + 1))
                    act.wait_ge(g_lo_done, b * (2 * HT) + q * NSLOT + (GF0 + t - 1))
                    nc.scalar.activation(gf[t % 2][:, :], bank[s], ACT.Gelu, bias=bias_ap).then_inc(gelu_done, 1)
                    act.wait_ge(gelu_done, b * (2 * HT) + q * NSLOT + (t + 1))
                    nc.scalar.copy(g_hl[s][:, 0, :], gf[t % 2][:, :]).then_inc(g_hi_done, 1)

                def w_hi(t, q, width, n):
                    s = t % NSLOT
                    act.wait_ge(s_raw[s], (b * (2 * HT // NSLOT) + q + (n + 1)) * 16)
                    act.wait_ge(w_slot_free, b * (2 * HT) + q * NSLOT + (t + 1))
                    nc.scalar.copy(w_hl[s][:, 0, 0:width], raw[s][:, 0:width]).then_inc(w_hi_done, 1)

                for t in range(PTILES):
                    w_hi(t, 0, W1, 0)
                with act.Fori(0, HT // NSLOT - 1) as q:
                    for j in range(NSLOT):
                        gelu(j, q, cb1[:, bass.ds(q * NSLOT + j, 1)])
                        w_hi(j + 3, q, W1, (j + 3) // NSLOT)
                for t in range(12, 16):
                    gelu(t, 0, cb1[:, t:t + 1])
                    w_hi(t + 3, 0, W1 if t + 3 < HT else W2, (t + 3) // NSLOT)
                for d in range(DT):
                    act.wait_ge(w_slot_free, b * (2 * HT) + (SLOTS0 + HT))
                    nc.scalar.activation(cms[:, 0, d, :], ACC[d], ACT.Identity,
                                         bias=cbias[:, bass.ds(b, 1), d]).then_inc(cms_hi_done, 1)
                with act.Fori(0, HT // NSLOT - 1) as q:
                    for j in range(NSLOT):
                        gelu(HT + j, q, mb1[:, bass.ds(q * NSLOT + j, 1)])
                        w_hi(HT + j + 3, q, W2, (HT + j + 3) // NSLOT)
                for t in range(28, 32):
                    gelu(t, 0, mb1[:, t - HT:t - HT + 1])
                    if t + 3 < 32:
                        w_hi(t + 3, 0, W2, (t + 3) // NSLOT)

            TOT = 2 * HT * B

            def y0_hi(b):
                act.wait_ge(y0_done, Y0 + (b + 1) * DT)
                for d in range(DT):
                    nc.scalar.copy(yT[b][:, 0, d, :], res[:, b, d, :]).then_inc(t_y0hi, 1)

            def z_norm(u, tiles=range(DT)):
                for i in tiles:
                    act.wait_ge(t_nmr, nmr_count(u, i))
                    nc.scalar.activation(z[u % 2][:, i, :], z[u % 2][:, i, :], ACT.Identity,
                                         scale=rstd[:, u % 2, i:i + 1], bias=nmr[:, u % 2, i:i + 1]).then_inc(t_zn, 1)

            def h_gelu(u):
                for m in range(MT):
                    act.wait_ge(t_down, u * MT + m + 1)
                    if m == 0:
                        act.wait_ge(t_pp[u % B], 16 * (u // B + 1))
                    if u > 0:
                        act.wait_ge(t_hlo, (u - 1) * MT + m + 1)
                    nc.scalar.activation(hf[m][:, :], down_bank(u, m), ACT.Gelu, bias=pp[:, u % B, 8 + m:9 + m]).then_inc(t_hf, 1)
                for m in range(MT):
                    act.wait_ge(t_hf, u * MT + m + 1)
                    if u >= 2:
                        act.wait_ge(t_up, (u - 1) * DT)
                    nc.scalar.copy(h_hl[u % 2][:, 0, m, :], hf[m][:, :]).then_inc(t_hhi, 1)

            def y_scale(u, tiles=range(DT)):
                for d in tiles:
                    act.wait_ge(t_tr, u * DT + d + 1)
                    if 1 <= u < 8:
                        act.wait_ge(t_ylo, (u - 1) * DT + d + 1)
                    dst = yf[d][:, :] if u < 8 else res[:, u % B, d, :]
                    nc.scalar.activation(dst, tr_bank(u, d), ACT.Identity,
                                         scale=pp[:, u % B, d:d + 1], bias=pp[:, u % B, 4 + d:5 + d]).then_inc(t_yf, 1)
                if u < 8:
                    for d in range(DT):
                        act.wait_ge(t_yf, u * DT + d + 1)
                        nc.scalar.copy(yT[u % B][:, 0, d, :], yf[d][:, :]).then_inc(t_yhi, 1)

            act.wait_ge(up_full, SLOTS0 + TOT)
            for b in range(B - 1):
                y0_hi(b)
            for s in range(12):
                if 2 <= s < 11:
                    z_norm(s - 2)
                h_gelu(s)
                if s == 11:
                    z_norm(9)
                if s == 0:
                    y0_hi(B - 1)
                if 2 <= s:
                    y_scale(s - 2)
            z_norm(10)
            y_scale(10)
            z_norm(11, (0, 2))
            y_scale(11, LAST_BY[0])

        @block.vector
        def _(dve):
            def lo_jobs(n, group, tile, scale=None, tiles=range(DT)):
                for m in tiles:
                    dve.wait_ge(act_done, n + (m + 1))
                    if scale is None:
                        nc.vector.tensor_tensor(tile[:, 1, m, :], bank[group + m], f(tile[:, 0, m, :]), ALU.subtract).then_inc(dve_done, 1)
                    else:
                        nc.vector.scalar_tensor_tensor(out=tile[:, 1, m, :], in0=bank[group + m], scalar=scale, in1=f(tile[:, 0, m, :]),
                                                       op0=ALU.mult, op1=ALU.subtract).then_inc(dve_done, 1)

            def x_lo_parts(seq):
                for k in range(DT):
                    dve.wait_ge(x_hi, seq * DT + (k + 1))
                    nc.vector.tensor_tensor(xT[:, 1, k, :], res[:, bass.ds(seq, 1), k, :].rearrange("p o n -> p (o n)"),
                                            f(xT[:, 0, k, :]), ALU.subtract).then_inc(x_split, 1)

            def softmax_jobs(n, seq):
                for m in range(DT):
                    dve.wait_ge(bank_full, n + (m + 1))
                    nc.vector.reduce_max(rowmax[:, m:m + 1], bank[LOW + m], AX.X).then_inc(s_rmax, 1)
                    dve.wait_ge(s_rmax, seq * DT + (m + 1))
                    nc.vector.tensor_scalar(negmax[:, m:m + 1], rowmax[:, m:m + 1], -1.0, None, ALU.mult).then_inc(s_nmax, 1)
                for m in range(DT):
                    dve.wait_ge(act_done, n + (m + 1))
                    nc.vector.reciprocal(rowinv[:, m:m + 1], rowsum[:, m:m + 1]).then_inc(s_rinv, 1)
                    dve.wait_ge(s_rinv, seq * DT + (m + 1))
                    nc.vector.tensor_scalar(probs[:, m, :], probs[:, m, :], rowinv[:, m:m + 1], None, ALU.mult).then_inc(dve_done, 1)

            def attn_lo(n, b):
                for m in range(DT):
                    dve.wait_ge(act_done, n + (m + 1))
                    hi, lo = (a_all[:, bass.ds(b, 1), e, m, :].rearrange("p o n -> p (o n)") for e in range(2))
                    nc.vector.scalar_tensor_tensor(out=lo, in0=bank[LOW + m], scalar=bp[:, m:m + 1], in1=f(hi),
                                                   op0=ALU.add, op1=ALU.subtract).then_inc(dve_done, 1)

            for n in range(2 * DT):
                w, raw_w = ((wqT, wq_raw), (wkT, wk_raw))[n % 2]
                dve.wait_ge(qk_hi, n + 1)
                nc.vector.tensor_tensor(w[:, 1, n // 2, :], raw_w[:, n // 2, :], f(w[:, 0, n // 2, :]), ALU.subtract).then_inc(qk_split, 1)
            x_lo_parts(0)
            lo_jobs(J_G, HIGH, g_w)
            for i, (w, raw_w) in enumerate(((wvT, wv_raw), (wp_s, wp_raw))):
                dve.wait_ge(s_whi[i], 1)
                nc.vector.tensor_tensor(w[:, 1, :, :], raw_w[:, :, :], f(w[:, 0, :, :]), ALU.subtract).then_inc(s_wsplit[i], 1)
            dve.wait_ge(s_bsum_in, 32)
            NS = (LAYERS - 1) * EXPERTS
            nc.vector.tensor_tensor(bsum[1][0:NS, :], bsum[1][0:NS, :], bsum[0][0:NS, :], ALU.add).then_inc(s_bsum, 1)
            lo_jobs(J_U0, LOW, uT, scale=SCALE)
            dve.wait_ge(s_small, 32)
            dve.wait_ge(s_iota, 1)
            nc.vector.tensor_copy(codes_f, codes_i[:, :]).then_inc(s_cast, 1)
            nc.vector.tensor_copy(feat_f, feat_i[:, :]).then_inc(s_cast, 1)
            dve.wait_ge(s_cast, 2)
            for b in range(B):
                nc.vector.scalar_tensor_tensor(out=cbias[:, b, :], in0=feat_f, scalar=codes_f[:, b:b + 1], in1=cb2,
                                               op0=ALU.is_equal, op1=ALU.add).then_inc(s_cbias, 1)
            lo_jobs(J_VP, HIGH, vp_w)
            softmax_jobs(J_S0, 0)
            with dve.Fori(0, B - 1) as b:
                n = b * PER
                lo_jobs(n + JV, LOW, v_n, tiles=(0, 1, 2))
                lo_jobs(n + JPT, HIGH, pT)
                lo_jobs(n + JV + DT, LOW, v_n, tiles=(3,))
                x_lo_parts(b + 1)
                attn_lo(n + JPV, b)
                lo_jobs(n + JU, HIGH, uT, scale=SCALE)
                softmax_jobs(n + JS, b + 1)
            lo_jobs(J_V3, LOW, v_n, tiles=(0, 1, 2))
            lo_jobs(J_PT3, HIGH, pT)
            lo_jobs(J_V3 + DT, LOW, v_n, tiles=(3,))
            for i in range(2):
                dve.wait_ge(p_free[i], 16 * (NPIECE // PSLOT + 1))
            for m in range(DT):
                dve.wait_ge(bank_full, J_PV3 + m + 1)
                src = ACC[m]
                nc.vector.tensor_scalar(a_all[:, B - 1, 0, m, :], src, bp[:, m:m + 1], None, ALU.add).then_inc(s_last_hi, 1)
                dve.wait_ge(s_last_hi, m + 1)
                nc.vector.scalar_tensor_tensor(out=a_all[:, B - 1, 1, m, :], in0=src, scalar=bp[:, m:m + 1], in1=f(a_all[:, B - 1, 0, m, :]),
                                               op0=ALU.add, op1=ALU.subtract).then_inc(y0_done, 1)

            with dve.Fori(0, B) as b:
                def seq_res(d):
                    return res[:, bass.ds(b, 1), d, :].rearrange("p o n -> p (o n)")

                def g_lo(t, q):
                    s = t % NSLOT
                    dve.wait_ge(g_hi_done, b * (2 * HT) + q * NSLOT + (t + 1))
                    nc.vector.tensor_tensor(g_hl[s][:, 1, :], gf[t % 2][:, :], f(g_hl[s][:, 0, :]), ALU.subtract).then_inc(g_lo_done, 1)

                def w_lo(t, q, width):
                    s = t % NSLOT
                    dve.wait_ge(w_hi_done, b * (2 * HT) + q * NSLOT + (t + 1))
                    nc.vector.tensor_tensor(w_hl[s][:, 1, 0:width], raw[s][:, 0:width], f(w_hl[s][:, 0, 0:width]), ALU.subtract).then_inc(w_lo_done, 1)

                with dve.Fori(0, HT // NSLOT - 1) as q:
                    for j in range(NSLOT):
                        g_lo(j, q)
                        w_lo(j + 3, q, W1)
                for t in range(12, 16):
                    g_lo(t, 0)
                    w_lo(t + 3, 0, W1 if t + 3 < HT else W2)
                for d in range(DT):
                    dve.wait_ge(cms_hi_done, b * DT + (d + 1))
                    nc.vector.scalar_tensor_tensor(out=cms[:, 1, d, :], in0=ACC[d], scalar=cbias[:, bass.ds(b, 1), d],
                                                   in1=f(cms[:, 0, d, :]), op0=ALU.add, op1=ALU.subtract).then_inc(cms_lo_done, 1)
                for d in range(DT):
                    nc.vector.scalar_tensor_tensor(out=seq_res(d), in0=ACC[d], scalar=cbias[:, bass.ds(b, 1), d],
                                                   in1=seq_res(d), op0=ALU.add, op1=ALU.add).then_inc(cms_added, 1)
                with dve.Fori(0, HT // NSLOT - 1) as q:
                    for j in range(NSLOT):
                        g_lo(HT + j, q)
                        w_lo(HT + j + 3, q, W2)
                for t in range(28, 32):
                    g_lo(t, 0)
                    if t + 3 < 32:
                        w_lo(t + 3, 0, W2)
                for d in range(DT):
                    dve.wait_ge(w_slot_free, b * (2 * HT) + (SLOTS0 + 2 * HT))
                    nc.vector.scalar_tensor_tensor(out=seq_res(d), in0=ACC[d], scalar=mb2[:, d:d + 1],
                                                   in1=seq_res(d), op0=ALU.add, op1=ALU.add).then_inc(mod_added, 1)
                for d in range(DT):
                    dve.wait_ge(mod_added, b * DT + (d + 1))
                    nc.vector.tensor_scalar(seq_res(d), seq_res(d), 0.0, 1.0, ALU.max, ALU.min).then_inc(y0_done, 1)

            def y0_rows(b):
                dve.wait_ge(t_bup0, 16 * B)
                dve.wait_ge(t_y0lo, (b + 1) * DT)
                dve.wait_ge(t_rows_full, (b + 1) * DT)
                for i in range(DT):
                    nc.vector.tensor_tensor(res[:, b, i, :], UP[i], bup0[:, b, :], ALU.add).then_inc(t_res_done, 1)

            def factors(u, k, n):
                dve.wait_ge(t_rstd, nmr_count(u, k))
                nc.vector.scalar_tensor_tensor(out=nmr[:, u % 2, k:k + n], in0=mv[:, u % 2, k:k + n, 0], scalar=-1.0,
                                               in1=rstd[:, u % 2, k:k + n], op0=ALU.mult, op1=ALU.mult).then_inc(t_nmr, 1)

            def h_lo(u):
                for m in range(MT):
                    dve.wait_ge(t_hhi, u * MT + m + 1)
                    nc.vector.tensor_tensor(h_hl[u % 2][:, 1, m, :], hf[m][:, :], f(h_hl[u % 2][:, 0, m, :]), ALU.subtract).then_inc(t_hlo, 1)

            def norm_tile(i):
                dve.wait_ge(t_nmr, nmr_count(11, i))
                nc.vector.tensor_scalar(z[1][:, i, :], z[1][:, i, :], rstd[:, 1, i:i + 1], nmr[:, 1, i:i + 1],
                                        ALU.mult, ALU.add).then_inc(t_znv, 1)

            def z_stats(u):
                for i in range(DT + 2):
                    if i < DT:
                        dve.wait_ge(t_up, u * DT + i + 1)
                        if u >= B:
                            dve.wait_ge(t_res, (u - B) * DT + i + 1)
                        if u >= 2:
                            if u < 10:
                                dve.wait_ge(t_rmul, (u - 2) * DT + i + 1)
                            dve.wait_ge(t_tr, (u - 1) * DT)
                        nc.vector.tensor_tensor(z[u % 2][:, i, :], UP[i], res[:, u % B, i, :], ALU.add).then_inc(t_z, 1)
                    if 1 <= i < DT + 1:
                        k = i - 1
                        dve.wait_ge(t_z, u * DT + k + 1)
                        if u >= 1:
                            dve.wait_ge(t_mv, (u - 1) * DT + k + 1)
                        nc.vector.bn_stats(stats[:, k, :], z[u % 2][:, k, :]).then_inc(t_bn, 1)
                    if i >= 2:
                        k = i - 2
                        dve.wait_ge(t_bn, u * DT + k + 1)
                        if k == 0 and u >= 2:
                            dve.wait_ge(t_nmr, nmr_count(u - 2, DT - 1))
                        nc.vector.bn_aggr(mv[:, u % 2, k, :], stats[:, k, :]).then_inc(t_mv, 1)
                    if i == DT and u >= FINE:
                        factors(u, 0, 2)
                if u == 11:
                    norm_tile(1)
                if u >= FINE:
                    factors(u, 2, 2)
                else:
                    factors(u, 0, DT)

            def y_lo(u):
                for d in range(DT):
                    dve.wait_ge(t_yhi, u * DT + d + 1)
                    nc.vector.tensor_tensor(yT[u % B][:, 1, d, :], yf[d][:, :], f(yT[u % B][:, 0, d, :]), ALU.subtract).then_inc(t_ylo, 1)

            def out_scale(u):
                for d in LAST_BY[1]:
                    dve.wait_ge(t_tr, u * DT + d + 1)
                    nc.vector.tensor_scalar(res[:, u % B, d, :], tr_bank(u, d), pp[:, u % B, d:d + 1], pp[:, u % B, 4 + d:5 + d],
                                            ALU.mult, ALU.add).then_inc(t_yv, 1)

            for s in range(13):
                if s == 0:
                    y0_rows(0)
                if s < 12:
                    h_lo(s)
                if s == 0:
                    y0_rows(1)
                if 1 <= s < 13:
                    z_stats(s - 1)
                if 1 <= s < 3:
                    y0_rows(s + 1)
                if 2 <= s < 10:
                    y_lo(s - 2)
            norm_tile(3)
            out_scale(11)

        @block.gpsimd
        def _(pool):
            nc.gpsimd.memset(ident[:, :], 0.0).then_inc(s_ident0, 1)
            pool.wait_ge(s_ident0, 1)
            nc.gpsimd.affine_select(out=ident[:, :], in_=ident[:, :], compare_op=ALU.not_equal, fill=1.0, base=0,
                                    pattern=[[-1, P]], channel_multiplier=1).then_inc(s_ident, 1)
            nc.gpsimd.iota(feat_i[:, :], pattern=[[P, DT]], base=0, channel_multiplier=1).then_inc(s_iota, 1)

            nc.gpsimd.memset(mhalf, -0.5).then_inc(s_half, 1)

            for i in range(PSLOT):
                nc.gpsimd.memset(sm[:, 192 + i:193 + i], 0.0).then_inc(p_free[i], 16)
            def piece_lo(phase, pieces):
                for c in pieces:
                    i = c % PSLOT
                    pool.wait_ge(p_hi, phase * PHASE + (c + 1))
                    nc.gpsimd.tensor_tensor(prep[i][:, 1, :], prep[i][:, 1, :], prep[i][:, 0, :], ALU.subtract).then_inc(p_lo, 1)

            piece_lo(0, range(PHASE))
            with pool.Fori(0, B - 1) as b:
                piece_lo(b + 1, range(PHASE))

            with pool.Fori(0, B) as b:
                for t in range(PTILES):
                    pool.wait_ge(w_hi_done, b * (2 * HT) + (t + 1))
                    nc.gpsimd.tensor_tensor(w_hl[t][:, 1, 0:W1], raw[t][:, 0:W1], f(w_hl[t][:, 0, 0:W1]), ALU.subtract).then_inc(w_lo_pool, 1)

            for b in range(B):
                for d in range(DT):
                    pool.wait_ge(t_y0hi, b * DT + d + 1)
                    nc.gpsimd.tensor_tensor(yT[b][:, 1, d, :], res[:, b, d, :], f(yT[b][:, 0, d, :]), ALU.subtract).then_inc(t_y0lo, 1)

            pool.wait_ge(s_half, 1)
            for u in range(12):
                i2 = u % 2
                for k, n in ((0, DT),) if u < FINE else ((0, 2), (2, 2)):
                    pool.wait_ge(t_mv, u * DT + k + n)
                    if u >= 2:
                        pool.wait_ge(t_zn, (u - 2) * DT + k + n)
                    nc.gpsimd.tensor_scalar(ve[:, i2, k:k + n], mv[:, i2, k:k + n, 1], EPS, 1.0, ALU.add, ALU.mult).then_inc(t_ve, 1)
                    pool.wait_ge(t_ve, nmr_count(u, k))
                    nc.gpsimd.tensor_tensor(rstd[:, i2, k:k + n], ve[:, i2, k:k + n], mhalf[:, 0:n], ALU.pow).then_inc(t_rstd, 1)
                if u >= 8:
                    continue
                pool.wait_ge(t_bc[i2], 32 * (u // 2 + 1))
                for i in range(DT):
                    pool.wait_ge(t_zn, u * DT + i + 1)
                    nc.gpsimd.tensor_tensor(res[:, u % B, i, :], z[i2][:, i, :], bc[i2][:, 0, :], ALU.mult).then_inc(t_rmul, 1)
                    pool.wait_ge(t_rmul, u * DT + i + 1)
                    nc.gpsimd.tensor_tensor(res[:, u % B, i, :], res[:, u % B, i, :], bc[i2][:, 1, :], ALU.add).then_inc(t_res, 1)


_OUT = "out_dram"


def kernel(**inputs):
    import numpy as np
    import concourse.bacc as bacc
    from concourse.bass_utils import run_bass_kernel_spmd

    a = {k: np.asarray(v) for k, v in inputs.items()}

    def rows(w):
        return np.ascontiguousarray(w.reshape(-1, P, w.shape[-1]).transpose(1, 0, 2))

    def cols(v):
        return v.reshape(-1, P).T

    def up_tiles(w):
        k, t = w.shape[0] // P, w.shape[1] // P
        return w.reshape(k, P, t, P).transpose(2, 1, 0, 3).reshape(t, P, k * P)

    wts = np.stack([rows(a["L0_cond_" + n]) if n == "Wp" else rows(a["L0_cond_" + n].T)
                    for n in ("Wv", "Wp", "Wq", "Wk")])
    mlp1 = np.concatenate([up_tiles(a["L0_cond_cW1"]), a["L0_cond_cW2"].reshape(HT, P, V)], axis=2)
    mlp2 = np.concatenate([up_tiles(a["L0_cond_mW1"]), a["L0_cond_mW2"].reshape(HT, P, V)], axis=2)
    bias = np.concatenate([cols(a["L0_cond_" + n]) for n in ("bp", "cb1", "cb2", "mb1", "mb2")], axis=1)
    names = [("L1", "ln_w", "ln_b"), ("L2", "gamma", "beta"), ("L3", "gamma", "beta")]
    wdu, pp, gb, bup = [], [], [], []
    for l, g, bt in names:
        for e in range(EXPERTS):
            w = np.concatenate([rows(a[f"{l}_cond_W_{n}"][e]).reshape(P, -1) for n in ("down", "up")], axis=1)
            wdu.append(w.reshape(P, NPC, PC).transpose(1, 0, 2))
            pp.append(np.concatenate([cols(a[f"{l}_cond_{g}"][e]), cols(a[f"{l}_cond_{bt}"][e]),
                                      cols(a[f"{l}_cond_b_down"][e])], axis=1))
            gb.append(np.stack([a[f"{l}_cond_{g}"][e], a[f"{l}_cond_{bt}"][e]]))
            bup.append(a[f"{l}_cond_b_up"][e])
    arrays = {
        "wts": wts, "x": np.stack([rows(a["x"][b].T) for b in range(B)]), "bias": bias,
        "codes": a["itok_B_17_1546"].reshape(1, B), "experts": a["itok_B_1_2"].reshape(1, B),
        "mlp1": mlp1, "mlp2": mlp2, "wdu": np.concatenate(wdu), "pp": np.stack(pp),
        "gb": np.stack(gb), "bup": np.stack(bup),
    }
    arrays = {k + "_dram": np.ascontiguousarray(v) for k, v in arrays.items()}
    nc = bacc.Bacc("TRN2", target_bir_lowering=False, num_devices=1)
    args = [nc.dram_tensor(k, v.shape, mybir.dt.from_np(v.dtype), kind="ExternalInput").ap()
            for k, v in arrays.items()]
    args.append(nc.dram_tensor(_OUT, (B, P, DT, S), F32, kind="ExternalOutput").ap())
    build(nc, *args)
    r = run_bass_kernel_spmd(nc, [arrays], core_ids=[0])
    got = r.results[0][_OUT]
    return np.ascontiguousarray(got.transpose(0, 3, 2, 1)).reshape(B, S, V)
```
